# Optimizing a Trainium2 kernel written in Bass

```python
import numpy as np
import jax
import jax.numpy as jnp

def _softmax(x, axis=-1):
    return jax.nn.softmax(x, axis=axis)

def _gelu(x):
    return jax.nn.gelu(x, approximate=True)

def _silu(x):
    return jax.nn.silu(x)

def _sigmoid(x):
    return jax.nn.sigmoid(x)

def _layernorm(x, axis=-1, eps=1e-05):
    m = jnp.mean(x, axis=axis, keepdims=True)
    v = jnp.var(x, axis=axis, keepdims=True)
    return (x - m) / jnp.sqrt(v + eps)

def _scatter_add(tgt, idx, src, axis=0):
    return tgt.at[idx].add(src)

def _segment_sum(src, seg, n):
    return jax.ops.segment_sum(src, seg, n)
kernel_name = 'mk_perceiver_d2_seqx_r4_a54205'

def setup_inputs(seed: int=0):
    np.random.seed(seed)
    _w = jnp.asarray

    def _rec_inputs():
        import jax
        import jax.numpy as jnp
        _rk = jax.random.key(seed)
        x = -0.0002928 + 1 * jax.random.normal(jax.random.fold_in(_rk, 1), (2, 64, 512), jnp.float32)
        _lenS = 64 - jax.random.randint(jax.random.fold_in(_rk, 7), (2,), 0, max(1, 64 // 4) + 1, jnp.int32)
        _lenS2 = 1024 - jax.random.randint(jax.random.fold_in(_rk, 8), (2,), 0, max(1, 1024 // 4) + 1, jnp.int32)
        _ctx_512P = jax.random.normal(jax.random.fold_in(_rk, 11), (2, 16, 128), jnp.float32)
        _ctx_512c = jax.random.dirichlet(jax.random.fold_in(_rk, 511), 0.3 * jnp.ones((16,), jnp.float32), (2, 1024))
        _ctx_512t = jnp.einsum('bsk,bkd->bsd', _ctx_512c, _ctx_512P)
        _ctx_512t = _ctx_512t * jax.lax.rsqrt(jnp.mean(jnp.square(_ctx_512t)) + 1e-12) * 0.953939
        ctx_512 = 0.000227908 + 0.99994 * (_ctx_512t + 0.3 * jax.random.normal(jax.random.fold_in(_rk, 611), (2, 1024, 128), jnp.float32))
        return (x, ctx_512)
    x, ctx_512 = _rec_inputs()

    def _L0_xattn_setup():
        import jax, jax.numpy as jnp
        import numpy as np
        B, S, L = (2, 256, 256)
        DIM_Q, H, K, D_C, D_CQ, R = (512, 16, 128, 128, 384, 64)

        def _rope_tables(seq_len, dim, dtype):
            inv_freq = 1.0 / 10000.0 ** (jnp.arange(0, dim, 2, dtype=dtype) / dim)
            t = jnp.arange(seq_len, dtype=dtype)
            freqs = t[:, None] * inv_freq[None, :]
            sin = jnp.repeat(jnp.sin(freqs), 2, axis=-1)
            cos = jnp.repeat(jnp.cos(freqs), 2, axis=-1)
            return (sin, cos)

        def _rotate_half(x):
            h = x.shape[-1] // 2
            return jnp.concatenate([-x[..., h:], x[..., :h]], axis=-1)
        key = jax.random.key(seed)
        ks = jax.random.split(key, 8)
        s_in = 1.0 / np.sqrt(DIM_Q)
        s_k = 1.0 / np.sqrt(K)
        s_cq = 1.0 / np.sqrt(D_CQ)
        s_c = 1.0 / np.sqrt(D_C)
        return {'hidden_q': jax.random.normal(ks[0], (B, S, DIM_Q), jnp.float32), 'kv_c': jax.random.normal(ks[1], (B, L, D_C), jnp.float32), 'Wq': jax.random.normal(ks[2], (H * K, DIM_Q), jnp.float32) * s_in, 'w_kc_q': jax.random.normal(ks[3], (H, K, D_CQ), jnp.float32) * s_k, 'w_kc_kv': jax.random.normal(ks[4], (H, K, D_C), jnp.float32) * s_k, 'W_qr': jax.random.normal(ks[5], (H, D_CQ, R), jnp.float32) * s_cq / np.sqrt(R), 'W_kr': jax.random.normal(ks[6], (H, D_C, R), jnp.float32) * s_c, 'Wo': jax.random.normal(ks[7], (DIM_Q, H * K), jnp.float32) * s_k}
    _L0_xattn_all = _L0_xattn_setup()
    _L0_xattn_in = {k: v for k, v in _L0_xattn_all.items() if k in ('Wq', 'w_kc_q', 'w_kc_kv', 'W_qr', 'W_kr', 'Wo')}
    del _L0_xattn_all

    def _L0_attn_setup():
        import jax, jax.numpy as jnp
        import numpy as np
        D_MODEL = 512
        NHEAD = 32
        N_KV = 8
        HEAD_DIM = D_MODEL // NHEAD
        EPS = 1e-05

        def weight_quant(w):
            scale = jnp.maximum(jnp.mean(jnp.abs(w)), EPS)
            return jax.lax.stop_gradient(jnp.sign(w) * scale - w) + w

        def bitlinear(x, w):
            return x @ weight_quant(w).T
        key = jax.random.key(seed)
        k1, k2, k3, k4, k5 = jax.random.split(key, 5)
        B, S = (2, 512)
        return {'x': jax.random.normal(k1, (B, S, D_MODEL), dtype=jnp.float32), 'wq': jax.random.normal(k2, (D_MODEL, D_MODEL), dtype=jnp.float32) * 0.02, 'wk': jax.random.normal(k3, (N_KV * HEAD_DIM, D_MODEL), dtype=jnp.float32) * 0.02, 'wv': jax.random.normal(k4, (N_KV * HEAD_DIM, D_MODEL), dtype=jnp.float32) * 0.02, 'wo': jax.random.normal(k5, (D_MODEL, D_MODEL), dtype=jnp.float32) * 0.02}
    _L0_attn_all = _L0_attn_setup()
    _L0_attn_in = {k: v for k, v in _L0_attn_all.items() if k in ('wq', 'wk', 'wv', 'wo')}
    del _L0_attn_all

    def _L0_ffn_setup():
        import jax, jax.numpy as jnp
        import numpy as np
        HIDDEN = 512
        INTER = 192
        N_EXPERTS = 32
        TOP_K = 8
        key = jax.random.key(seed)
        k = jax.random.split(key, 5)
        s = 1.0 / np.sqrt(HIDDEN)
        return {'hidden_states': jax.random.normal(k[0], (1, 256, HIDDEN), jnp.float32), 'gate_w': jax.random.normal(k[1], (HIDDEN, N_EXPERTS), jnp.float32) * s, 'w_gate': jax.random.normal(k[2], (N_EXPERTS, HIDDEN, INTER), jnp.float32) * s, 'w_up': jax.random.normal(k[3], (N_EXPERTS, HIDDEN, INTER), jnp.float32) * s, 'w_down': jax.random.normal(k[4], (N_EXPERTS, INTER, HIDDEN), jnp.float32) * (1.0 / np.sqrt(INTER))}
    _L0_ffn_all = _L0_ffn_setup()
    _L0_ffn_in = {k: v for k, v in _L0_ffn_all.items() if k in ('gate_w', 'w_gate', 'w_up', 'w_down')}
    del _L0_ffn_all

    def _L1_xattn_setup():
        import jax, jax.numpy as jnp
        import numpy as np
        B, S, H, NH, L = (2, 512, 512, 16, 128)
        HD = H // NH
        key = jax.random.key(seed)
        k1, k2, k3, k4, k5 = jax.random.split(key, 5)
        scale = 0.02
        return {'q': jax.random.normal(k1, (B, S, H), dtype=jnp.float32), 'latent_kv': jax.random.normal(k2, (B, S, L), dtype=jnp.float32), 'Wq': jax.random.normal(k3, (H, H), dtype=jnp.float32) * scale, 'Wkv_expand': jax.random.normal(k4, (2 * H, L), dtype=jnp.float32) * scale, 'Wout': jax.random.normal(k5, (H, H), dtype=jnp.float32) * scale}
    _L1_xattn_all = _L1_xattn_setup()
    _L1_xattn_in = {k: v for k, v in _L1_xattn_all.items() if k in ('Wq', 'Wkv_expand', 'Wout')}
    del _L1_xattn_all

    def _L1_attn_setup():
        import jax, jax.numpy as jnp
        import numpy as np
        NHEADS = 16
        SCALE_BASE = 512.0
        EPS = 1e-05

        def _rotate_every_two(x):
            x1 = x[..., ::2]
            x2 = x[..., 1::2]
            return jnp.stack([-x2, x1], axis=-1).reshape(x.shape)

        def _xpos(x, offset=0):
            B, T, C = x.shape
            dim_scale = (jnp.arange(0, C, 2, dtype=jnp.float32) + 0.4 * C) / (1.4 * C)
            pos = jnp.arange(offset, offset + T, dtype=jnp.float32)
            scale = dim_scale[None, :] ** (pos[:, None] / SCALE_BASE)
            inv_freq = 1.0 / 10000.0 ** (jnp.arange(0, C, 2, dtype=jnp.float32) / C)
            sinusoid = pos[:, None] * inv_freq[None, :]
            sin = jnp.repeat(jnp.sin(sinusoid) * scale, 2, axis=-1)
            cos = jnp.repeat(jnp.cos(sinusoid) * scale, 2, axis=-1)
            return x * cos[None] + _rotate_every_two(x) * sin[None]

        def _decay_mask(H, T, dtype):
            gamma = 1.0 - 2.0 ** (-5.0 - jnp.arange(H, dtype=jnp.float32))
            idx = jnp.arange(T)
            diff = idx[:, None] - idx[None, :]
            exp = jnp.where(diff >= 0, diff, 0).astype(jnp.float32)
            mask = jnp.where(diff[None] >= 0, gamma[:, None, None] ** exp[None], 0.0)
            return (mask.astype(dtype), gamma)
        key = jax.random.key(seed)
        ks = jax.random.split(key, 4)
        B, T, C = (4, 256, 512)
        s = 0.02
        return {'x': jax.random.normal(ks[0], (B, T, C), dtype=jnp.float32), 'w_qkv': jax.random.normal(ks[1], (C, 3 * C), dtype=jnp.float32) * s, 'w_g': jax.random.normal(ks[2], (C, C), dtype=jnp.float32) * s, 'w_proj': jax.random.normal(ks[3], (C, C), dtype=jnp.float32) * s, 'gn_weight': jnp.ones((C,), dtype=jnp.float32), 'gn_bias': jnp.zeros((C,), dtype=jnp.float32)}
    _L1_attn_all = _L1_attn_setup()
    _L1_attn_in = {k: v for k, v in _L1_attn_all.items() if k in ('w_qkv', 'w_g', 'w_proj', 'gn_weight', 'gn_bias')}
    del _L1_attn_all

    def _L1_ffn_setup():
        import jax, jax.numpy as jnp
        import numpy as np
        H = 512
        I = 256
        K = 8
        E = 128
        TOPK = 4
        EPS = 1e-08
        key = jax.random.key(seed)
        ks = jax.random.split(key, 10)
        s = 0.02
        return {'x': jax.random.normal(ks[0], (4, 512, H), jnp.float32), 'w_router': jax.random.normal(ks[1], (H, E), jnp.float32) * s, 'w_gate': jax.random.normal(ks[2], (H, K * I), jnp.float32) * s, 'w_up': jax.random.normal(ks[3], (H, K * I), jnp.float32) * s, 'w_down': jax.random.normal(ks[4], (I, H), jnp.float32) * s, 'amplitudes': jax.random.normal(ks[5], (E, K, 2), jnp.float32) * 0.1, 'expert_scale': jnp.ones((E,), jnp.float32), 'shared_w_gate': jax.random.normal(ks[6], (H, 2 * I), jnp.float32) * s, 'shared_w_up': jax.random.normal(ks[7], (H, 2 * I), jnp.float32) * s, 'shared_w_down': jax.random.normal(ks[8], (2 * I, H), jnp.float32) * s}
    _L1_ffn_all = _L1_ffn_setup()
    _L1_ffn_in = {k: v for k, v in _L1_ffn_all.items() if k in ('w_router', 'w_gate', 'w_up', 'w_down', 'amplitudes', 'expert_scale', 'shared_w_gate', 'shared_w_up', 'shared_w_down')}
    del _L1_ffn_all
    return {'x': x, 'ctx_512': ctx_512, 'L0_xattn_Wq': _L0_xattn_in['Wq'], 'L0_xattn_w_kc_q': _L0_xattn_in['w_kc_q'], 'L0_xattn_w_kc_kv': _L0_xattn_in['w_kc_kv'], 'L0_xattn_W_qr': _L0_xattn_in['W_qr'], 'L0_xattn_W_kr': _L0_xattn_in['W_kr'], 'L0_xattn_Wo': _L0_xattn_in['Wo'], 'L0_attn_wq': _L0_attn_in['wq'], 'L0_attn_wk': _L0_attn_in['wk'], 'L0_attn_wv': _L0_attn_in['wv'], 'L0_attn_wo': _L0_attn_in['wo'], 'L0_ffn_gate_w': _L0_ffn_in['gate_w'], 'L0_ffn_w_gate': _L0_ffn_in['w_gate'], 'L0_ffn_w_up': _L0_ffn_in['w_up'], 'L0_ffn_w_down': _L0_ffn_in['w_down'], 'L1_xattn_Wq': _L1_xattn_in['Wq'], 'L1_xattn_Wkv_expand': _L1_xattn_in['Wkv_expand'], 'L1_xattn_Wout': _L1_xattn_in['Wout'], 'L1_attn_w_qkv': _L1_attn_in['w_qkv'], 'L1_attn_w_g': _L1_attn_in['w_g'], 'L1_attn_w_proj': _L1_attn_in['w_proj'], 'L1_attn_gn_weight': _L1_attn_in['gn_weight'], 'L1_attn_gn_bias': _L1_attn_in['gn_bias'], 'L1_ffn_w_router': _L1_ffn_in['w_router'], 'L1_ffn_w_gate': _L1_ffn_in['w_gate'], 'L1_ffn_w_up': _L1_ffn_in['w_up'], 'L1_ffn_w_down': _L1_ffn_in['w_down'], 'L1_ffn_amplitudes': _L1_ffn_in['amplitudes'], 'L1_ffn_expert_scale': _L1_ffn_in['expert_scale'], 'L1_ffn_shared_w_gate': _L1_ffn_in['shared_w_gate'], 'L1_ffn_shared_w_up': _L1_ffn_in['shared_w_up'], 'L1_ffn_shared_w_down': _L1_ffn_in['shared_w_down']}

def reference(x, ctx_512, L0_xattn_Wq, L0_xattn_w_kc_q, L0_xattn_w_kc_kv, L0_xattn_W_qr, L0_xattn_W_kr, L0_xattn_Wo, L0_attn_wq, L0_attn_wk, L0_attn_wv, L0_attn_wo, L0_ffn_gate_w, L0_ffn_w_gate, L0_ffn_w_up, L0_ffn_w_down, L1_xattn_Wq, L1_xattn_Wkv_expand, L1_xattn_Wout, L1_attn_w_qkv, L1_attn_w_g, L1_attn_w_proj, L1_attn_gn_weight, L1_attn_gn_bias, L1_ffn_w_router, L1_ffn_w_gate, L1_ffn_w_up, L1_ffn_w_down, L1_ffn_amplitudes, L1_ffn_expert_scale, L1_ffn_shared_w_gate, L1_ffn_shared_w_up, L1_ffn_shared_w_down):
    import jax
    import jax.numpy as jnp

    def _L0_xattn_ref(hidden_q, kv_c, Wq, w_kc_q, w_kc_kv, W_qr, W_kr, Wo):
        import jax, jax.numpy as jnp
        import numpy as np
        B, S, L = (2, 256, 256)
        DIM_Q, H, K, D_C, D_CQ, R = (512, 16, 128, 128, 384, 64)

        def _rope_tables(seq_len, dim, dtype):
            inv_freq = 1.0 / 10000.0 ** (jnp.arange(0, dim, 2, dtype=dtype) / dim)
            t = jnp.arange(seq_len, dtype=dtype)
            freqs = t[:, None] * inv_freq[None, :]
            sin = jnp.repeat(jnp.sin(freqs), 2, axis=-1)
            cos = jnp.repeat(jnp.cos(freqs), 2, axis=-1)
            return (sin, cos)

        def _rotate_half(x):
            h = x.shape[-1] // 2
            return jnp.concatenate([-x[..., h:], x[..., :h]], axis=-1)
        b, s, _ = hidden_q.shape
        l = kv_c.shape[1]
        q_hk = (hidden_q @ Wq.T).reshape(b, s, H, K)
        q_big = jnp.einsum('bshk,hkq->bshq', q_hk, w_kc_q)
        sin, cos = _rope_tables(l, D_C, kv_c.dtype)
        kv_rope = kv_c * cos[None] + _rotate_half(kv_c) * sin[None]
        q_r = jnp.einsum('bshq,hqr->bhsr', q_big, W_qr)
        k_r = jnp.einsum('bld,hdr->bhlr', kv_rope, W_kr)
        scores = jnp.einsum('bhsr,bhlr->bhsl', q_r, k_r)
        attn = jax.nn.softmax(scores, axis=-1)
        ctx_c = jnp.einsum('bhsl,bld->bhsd', attn, kv_rope)
        ctx_lat = jnp.einsum('bhsd,hkd->bshk', ctx_c, w_kc_kv)
        out = ctx_lat.reshape(b, s, H * K) @ Wo.T
        return out

    def _L0_attn_ref(x, wq, wk, wv, wo):
        import jax, jax.numpy as jnp
        import numpy as np
        D_MODEL = 512
        NHEAD = 32
        N_KV = 8
        HEAD_DIM = D_MODEL // NHEAD
        EPS = 1e-05

        def weight_quant(w):
            scale = jnp.maximum(jnp.mean(jnp.abs(w)), EPS)
            return jax.lax.stop_gradient(jnp.sign(w) * scale - w) + w

        def bitlinear(x, w):
            return x @ weight_quant(w).T
        B, S, _ = x.shape
        G = NHEAD // N_KV
        q = bitlinear(x, wq).reshape(B, S, N_KV, G, HEAD_DIM)
        k = bitlinear(x, wk).reshape(B, S, N_KV, HEAD_DIM)
        v = bitlinear(x, wv).reshape(B, S, N_KV, HEAD_DIM)
        sm_scale = 1.0 / jnp.sqrt(jnp.asarray(HEAD_DIM, dtype=x.dtype))
        scores = jnp.einsum('bskgd,btkd->bkgst', q, k) * sm_scale
        causal = jnp.tril(jnp.ones((S, S), dtype=bool))
        scores = jnp.where(causal, scores, jnp.asarray(-jnp.inf, dtype=scores.dtype))
        probs = jax.nn.softmax(scores, axis=-1)
        out = jnp.einsum('bkgst,btkd->bskgd', probs, v)
        out = out.reshape(B, S, D_MODEL)
        return bitlinear(out, wo)

    def _L0_ffn_ref(hidden_states, gate_w, w_gate, w_up, w_down):
        import jax, jax.numpy as jnp
        import numpy as np
        HIDDEN = 512
        INTER = 192
        N_EXPERTS = 32
        TOP_K = 8
        B, S, H = hidden_states.shape
        E = gate_w.shape[1]
        x = hidden_states.reshape(-1, H)
        T = x.shape[0]
        K = TOP_K
        P = T * K
        C = 2 * (P // E)
        probs = jax.nn.softmax(x @ gate_w, axis=-1)
        w, sel = jax.lax.top_k(probs, K)
        w = w / jnp.sum(w, axis=-1, keepdims=True)
        flat_e = sel.reshape(-1)
        flat_t = jnp.repeat(jnp.arange(T), K)
        flat_w = w.reshape(-1)
        order = jnp.argsort(flat_e)
        se = flat_e[order]
        start = jnp.searchsorted(se, jnp.arange(E))
        pos = jnp.arange(P) - start[se]
        slot = jnp.where(pos < C, se * C + pos, E * C)
        slot_pair = jnp.full((E * C,), P, dtype=jnp.int32).at[slot].set(order.astype(jnp.int32), mode='drop')
        t_slot = jnp.concatenate([flat_t, jnp.array([T])])[slot_pair]
        w_slot = jnp.concatenate([flat_w, jnp.zeros((1,), flat_w.dtype)])[slot_pair]
        x_pad = jnp.concatenate([x, jnp.zeros((1, H), x.dtype)], axis=0)
        xg = x_pad[t_slot].reshape(E, C, H)
        g = jnp.einsum('ech,ehi->eci', xg, w_gate)
        u = jnp.einsum('ech,ehi->eci', xg, w_up)
        y = jnp.einsum('eci,eih->ech', jax.nn.silu(g) * u, w_down).reshape(E * C, H)
        out = jnp.zeros((T + 1, H), x.dtype).at[t_slot].add(w_slot[:, None] * y)
        return out[:T].reshape(B, S, H)

    def _L1_xattn_ref(q, latent_kv, Wq, Wkv_expand, Wout):
        import jax, jax.numpy as jnp
        import numpy as np
        B, S, H, NH, L = (2, 512, 512, 16, 128)
        HD = H // NH
        b, sq, _ = q.shape
        sk = latent_kv.shape[1]
        qp = q @ Wq.T
        kv = latent_kv @ Wkv_expand.T
        k, v = jnp.split(kv, 2, axis=-1)
        qh = qp.reshape(b, sq, NH, HD).transpose(0, 2, 1, 3)
        kh = k.reshape(b, sk, NH, HD).transpose(0, 2, 1, 3)
        vh = v.reshape(b, sk, NH, HD).transpose(0, 2, 1, 3)
        inv_sqrt_d = 1.0 / jnp.sqrt(jnp.float32(HD))
        scores = jnp.einsum('bhqd,bhkd->bhqk', qh, kh) * inv_sqrt_d
        causal = jnp.tril(jnp.ones((sq, sk), dtype=bool))
        scores = jnp.where(causal, scores, jnp.finfo(scores.dtype).min)
        attn = jax.nn.softmax(scores, axis=-1)
        out = jnp.einsum('bhqk,bhkd->bhqd', attn, vh)
        out = out.transpose(0, 2, 1, 3).reshape(b, sq, H)
        return out @ Wout.T

    def _L1_attn_ref(x, w_qkv, w_g, w_proj, gn_weight, gn_bias):
        import jax, jax.numpy as jnp
        import numpy as np
        NHEADS = 16
        SCALE_BASE = 512.0
        EPS = 1e-05

        def _rotate_every_two(x):
            x1 = x[..., ::2]
            x2 = x[..., 1::2]
            return jnp.stack([-x2, x1], axis=-1).reshape(x.shape)

        def _xpos(x, offset=0):
            B, T, C = x.shape
            dim_scale = (jnp.arange(0, C, 2, dtype=jnp.float32) + 0.4 * C) / (1.4 * C)
            pos = jnp.arange(offset, offset + T, dtype=jnp.float32)
            scale = dim_scale[None, :] ** (pos[:, None] / SCALE_BASE)
            inv_freq = 1.0 / 10000.0 ** (jnp.arange(0, C, 2, dtype=jnp.float32) / C)
            sinusoid = pos[:, None] * inv_freq[None, :]
            sin = jnp.repeat(jnp.sin(sinusoid) * scale, 2, axis=-1)
            cos = jnp.repeat(jnp.cos(sinusoid) * scale, 2, axis=-1)
            return x * cos[None] + _rotate_every_two(x) * sin[None]

        def _decay_mask(H, T, dtype):
            gamma = 1.0 - 2.0 ** (-5.0 - jnp.arange(H, dtype=jnp.float32))
            idx = jnp.arange(T)
            diff = idx[:, None] - idx[None, :]
            exp = jnp.where(diff >= 0, diff, 0).astype(jnp.float32)
            mask = jnp.where(diff[None] >= 0, gamma[:, None, None] ** exp[None], 0.0)
            return (mask.astype(dtype), gamma)
        B, T, C = x.shape
        H = NHEADS
        D = C // H
        qkv = x @ w_qkv
        q, k, v = jnp.split(qkv, 3, axis=-1)
        q = _xpos(q, offset=0)
        k = _xpos(k, offset=0)
        q = q.reshape(B, T, H, D).transpose(0, 2, 1, 3)
        k = k.reshape(B, T, H, D).transpose(0, 2, 1, 3)
        v = v.reshape(B, T, H, D).transpose(0, 2, 1, 3)
        mask, _ = _decay_mask(H, T, x.dtype)
        scores = jnp.einsum('bhtd,bhsd->bhts', q, k) * D ** (-0.5)
        scores = scores * mask[None]
        y = jnp.einsum('bhts,bhsd->bhtd', scores, v)
        yg = y.transpose(0, 2, 1, 3).reshape(B * T, H, D)
        mu = jnp.mean(yg, axis=-1, keepdims=True)
        var = jnp.var(yg, axis=-1, keepdims=True)
        yn = (yg - mu) / jnp.sqrt(var + EPS)
        yn = yn.reshape(B * T, C) * gn_weight[None] + gn_bias[None]
        yn = yn.reshape(B, T, C)
        out = jax.nn.silu(x @ w_g) * yn
        return out @ w_proj

    def _L1_ffn_ref(x, w_router, w_gate, w_up, w_down, amplitudes, expert_scale, shared_w_gate, shared_w_up, shared_w_down):
        import jax, jax.numpy as jnp
        import numpy as np
        H = 512
        I = 256
        K = 8
        E = 128
        TOPK = 4
        EPS = 1e-08
        B, S, _ = x.shape
        T = B * S
        xt = x.reshape(T, H)
        probs = jax.nn.softmax(xt @ w_router, axis=-1)
        topk_p, topk_idx = jax.lax.top_k(probs, TOPK)
        topk_w = topk_p / (jnp.sum(topk_p, axis=-1, keepdims=True) + EPS)
        gate = (xt @ w_gate).reshape(T, K, I)
        up = (xt @ w_up).reshape(T, K, I)
        basis = jax.nn.silu(gate) * up
        p = amplitudes[..., 0] ** 2 + amplitudes[..., 1] ** 2
        mix = p / (jnp.sum(p, axis=-1, keepdims=True) + EPS)
        mix_sel = mix[topk_idx]
        mixed = jnp.einsum('tek,tki->tei', mix_sel, basis)
        down = jnp.einsum('tei,ih->teh', mixed, w_down)
        coeff = topk_w * expert_scale[topk_idx]
        out = jnp.einsum('teh,te->th', down, coeff)
        shared = jax.nn.silu(xt @ shared_w_gate) * (xt @ shared_w_up) @ shared_w_down
        out = out + shared
        return out.reshape(B, S, H)
    x = x + _L0_xattn_ref(_layernorm(x, axis=-1), ctx_512, L0_xattn_Wq, L0_xattn_w_kc_q, L0_xattn_w_kc_kv, L0_xattn_W_qr, L0_xattn_W_kr, L0_xattn_Wo)
    x = x + _L0_attn_ref(_layernorm(x, axis=-1), L0_attn_wq, L0_attn_wk, L0_attn_wv, L0_attn_wo)
    x = x + _L0_ffn_ref(_layernorm(x, axis=-1), L0_ffn_gate_w, L0_ffn_w_gate, L0_ffn_w_up, L0_ffn_w_down)
    x = x + _L1_xattn_ref(_layernorm(x, axis=-1), ctx_512, L1_xattn_Wq, L1_xattn_Wkv_expand, L1_xattn_Wout)
    x = x + _L1_attn_ref(_layernorm(x, axis=-1), L1_attn_w_qkv, L1_attn_w_g, L1_attn_w_proj, L1_attn_gn_weight, L1_attn_gn_bias)
    x = x + _L1_ffn_ref(_layernorm(x, axis=-1), L1_ffn_w_router, L1_ffn_w_gate, L1_ffn_w_up, L1_ffn_w_down, L1_ffn_amplitudes, L1_ffn_expert_scale, L1_ffn_shared_w_gate, L1_ffn_shared_w_up, L1_ffn_shared_w_down)
    return x

_drawn_inputs = setup_inputs


def setup_inputs(seed=0):
    import zlib

    import numpy as np

    out = dict(_drawn_inputs(seed))
    spreads = {'L1_attn_gn_weight': (1.0, 0.6),
     'L1_attn_gn_bias': (0.0, 0.8),
     'L1_ffn_expert_scale': (1.0, 0.6)}
    factors = {'L0_attn_wq': 8.0,
     'L0_attn_wk': 8.0,
     'L1_xattn_Wq': 24.163,
     'L1_ffn_w_router': 8.0,
     'L1_ffn_w_gate': 6.092,
     'L1_ffn_w_up': 6.091,
     'L1_ffn_w_down': 6.029,
     'L1_ffn_amplitudes': 8.0,
     'L1_ffn_shared_w_gate': 7.506,
     'L1_ffn_shared_w_up': 7.464,
     'L1_ffn_shared_w_down': 7.343}
    for name, (base, spread) in spreads.items():
        noise = np.random.default_rng([zlib.crc32(name.encode()), seed]).standard_normal(out[name].shape)
        drawn = base * np.exp(spread * noise) if base else spread * noise
        out[name] = jnp.asarray(drawn.astype(out[name].dtype))
    for name, factor in factors.items():
        out[name] = (out[name] * factor).astype(out[name].dtype)
    return out
```

```python
from contextlib import ExitStack

import numpy as np
import concourse.bass as bass
from concourse import mybir

F32 = mybir.dt.float32
BF16 = mybir.dt.bfloat16
U32 = mybir.dt.uint32
ALU = mybir.AluOpType
ACT = mybir.ActivationFunctionType
AX = mybir.AxisListType

P = 128
B, S, D = 2, 64, 512
C = D // P
L = 1024
H0, R0, DQ = 16, 64, 384
KQ = DQ // P
GROUPS = H0 // 4
UNITS = H0 * S * B // P
J = L // P
E0, I0, CAP = 32, 192, 64
PAIRS = E0 // 2
SLOTS = 4
EPS = 1e-5

PAIR_GU = 2 * C * I0
PAIR_N = 2 * PAIR_GU + 3 * D

A_G = C * 512 + 4 * KQ * P + 4 * KQ * R0
A_N = GROUPS * A_G
B_N = H0 * D + H0 * P
D_N = 19968

K_ID, K_MASK, K_U, K_IOTA, K_M16, K_M32, K_N = 0, 128, 256, 384, 512, 520, 524


def build(nc, x_in, consts_d, rope_d, ctx_d, ctx64_d, wa_d, wkr_d, wb_d, e0_d, gatew_d, ring_d, e1_d, b1_d,
          xpos_d, gn_d, decay_d, f1gu_d, f1s_d, f1d_d, router_d, escale_d, amp_d, out_d):
    with ExitStack() as stack:
        def sb(name, shape, dt=F32):
            return stack.enter_context(nc.sbuf_tensor(name, shape, dt))

        def sem(name):
            return stack.enter_context(nc.semaphore(name))

        ra = sb("ra", [P, A_N])
        rb = sb("rb", [P, B_N])
        rd = sb("rd", [P, D_N])
        x = sb("x", [P, D])
        xn = sb("xn", [P, D])
        xnT = sb("xnT", [P, C, P])
        cst = sb("cst", [P, K_N])
        identb = sb("identb", [P, P], BF16)
        maskb = sb("maskb", [P, 4, P], BF16)
        ones = sb("ones", [P, P])
        xpos = sb("xpos", [P, 2, D])
        gnwb = sb("gnwb", [P, 2, D])
        ctx64 = sb("ctx64", [P, P])
        ctx64T = sb("ctx64T", [P, P])
        gatew = sb("gatew", [P, C, E0])
        escale = sb("escale", [P, P])
        amp = sb("amp", [P, 8, 2])
        sv = sb("sv", [P, 332])
        top8i = sb("top8i", [P, 8], U32)
        ps = stack.enter_context(nc.psum_tensor("ps", [P, 8, 512], F32))

        ident = cst[:, K_ID:K_ID + P]
        maskf = cst[:, K_MASK:K_MASK + P]
        upper = cst[:, K_U:K_U + P]
        iota = cst[:, K_IOTA:K_IOTA + P]
        m16 = cst[:, K_M16:K_M16 + 8]
        m32 = cst[:, K_M32:K_M32 + 4]

        def wq_x(g):
            return ra[:, g * A_G:g * A_G + 2048].rearrange("p (c n) -> p c n", c=C)

        def wkcq(g):
            o = g * A_G + 2048
            return ra[:, o:o + 1536].rearrange("p (h c k) -> p h c k", h=4, c=KQ)

        def wqr(g):
            o = g * A_G + 3584
            return ra[:, o:o + 768].rearrange("p (h c r) -> p h c r", h=4, c=KQ)

        wo_x = rb[:, 0:8192].rearrange("p (h n) -> p h n", h=H0)
        wkv_x = rb[:, 8192:10240].rearrange("p (h k) -> p h k", h=H0)
        ctxr = rd[:, 0:2048].rearrange("p (b j d) -> p b j d", b=B, j=J)
        rope_cos = rd[:, 2048:3072].rearrange("p (j d) -> p j d", j=J)
        rope_sin = rd[:, 3072:4096].rearrange("p (j d) -> p j d", j=J)
        rope_tmp = rd[:, 4096:5120].rearrange("p (j d) -> p j d", j=J)
        qT_x = rd[:, 5120:7168].rearrange("p (h t) -> p h t", h=H0)
        qrk = rd[:, 7168:9216].rearrange("p (h k) -> p h k", h=H0)
        qkw = rd[:, 9216:11264].rearrange("p (h d) -> p h d", h=H0)
        wkrT = rd[:, 11264:13312].rearrange("p (h d) -> p h d", h=H0)
        kvr = rd[:, 13824:15872].rearrange("p (b j d) -> p b j d", b=B, j=J)
        kvT = rd[:, 15872:17920].rearrange("p (b l) -> p b l", b=B)
        qk_x = rd[:, 17920:19968].rearrange("p (b h s) -> p b h s", b=B, h=H0)
        prob_x = [ra[:, 1024 * i:1024 * i + 1024].rearrange("p (j l) -> p j l", j=J) for i in range(2)]
        probT_x = [ra[:, 2048 + 1024 * i:3072 + 1024 * i].rearrange("p (j r) -> p j r", j=J) for i in range(2)]
        ctxT = ra[:, 4096:6144].rearrange("p (h b s) -> p h b s", h=H0, b=B)
        latT = ra[:, 11264:13312].rearrange("p (h t) -> p h t", h=H0)
        we = ra[:, 6144:11264]
        e_wq = we[:, 0:2048].rearrange("p (c n) -> p c n", c=C)
        e_wk0 = we[:, 2048:2560].rearrange("p (c n) -> p c n", c=C)
        e_wv0 = we[:, 2560:3072].rearrange("p (c n) -> p c n", c=C)
        e_wk1 = we[:, 2048:2560]
        e_wv1 = we[:, 2560:3072]
        e_wo = we[:, 3072:5120].rearrange("p (c n) -> p c n", c=C)
        att_banks = [8, 4]
        att_hd = [16, 32]
        att_prob = [ra[:, 0:4096].rearrange("p (i h t) -> p i h t", i=8, h=4),
                    ra[:, 0:2048].rearrange("p (i h t) -> p i h t", i=4, h=4)]
        att_probT = [rb[:, 0:4096].rearrange("p (i h t) -> p i h t", i=8, h=4),
                     ra[:, 2048:4096].rearrange("p (i h t) -> p i h t", i=4, h=4)]
        att_kbd = [ra[:, 4096:5120].rearrange("p (h t) -> p h t", h=8),
                   ra[:, 4096:6144].rearrange("p (h t) -> p h t", h=16)]
        att_qT = [ra[:, 5120:5632].rearrange("p (i t) -> p i t", i=4),
                  ra[:, 11856:12368].rearrange("p (i t) -> p i t", i=4)]
        att_v = [ra[:, 5632:5848], ra[:, 11264:11856]]
        att_o = [rb[:, 4096:4608], ra[:, 12368:12880]]
        att_oT = [rb[:, 4608:5120].rearrange("p (c t) -> p c t", c=C),
                  ra[:, 11856:12368].rearrange("p (c t) -> p c t", c=C)]
        slot = [rd[:, PAIR_N * j:PAIR_N * (j + 1)] for j in range(SLOTS)]
        slot_gate = [s[:, 0:PAIR_GU].rearrange("p (e c n) -> p e c n", e=2, c=C) for s in slot]
        slot_up = [s[:, PAIR_GU:2 * PAIR_GU].rearrange("p (e c n) -> p e c n", e=2, c=C) for s in slot]
        slot_down = [s[:, 2 * PAIR_GU:PAIR_N].rearrange("p (c n) -> p c n", c=3) for s in slot]
        moe_th = [ra[:, 384 * i:384 * i + 384] for i in range(2)]
        moe_a = ra[:, 768:1152]
        moe_h = [ra[:, 1152 + 384 * i:1536 + 384 * i] for i in range(2)]
        moe_hT = [ra[:, 1920 + 384 * i:2304 + 384 * i].rearrange("p (c t) -> p c t", c=3) for i in range(2)]
        w_ret = rb[:, 0:8192].rearrange("p (c t n) -> p c t n", c=C, t=4)
        w_proj = rb[:, 8192:10240].rearrange("p (c n) -> p c n", c=C)
        rot = ra[:, 0:1024].rearrange("p (t n) -> p t n", t=2)
        rot_tmp = ra[:, 1024:2048].rearrange("p (t n) -> p t n", t=2)
        ret_v = ra[:, 2048:2624]
        ret_kT = ra[:, 2624:3136].rearrange("p (c t) -> p c t", c=C)
        ret_th = ra[:, 3136:3648]
        ret_ag = ra[:, 3648:4160]
        ret_qbd = ra[:, 4160:6208].rearrange("p (c h t) -> p c h t", c=C, h=4)
        ret_pT = ra[:, 6208:8256].rearrange("p (c h t) -> p c h t", c=C, h=4)
        ret_y = ra[:, 8256:8768].rearrange("p (h d) -> p h d", h=16)
        ret_sq = ra[:, 8768:9280].rearrange("p (h d) -> p h d", h=16)
        ret_oT = ra[:, 9280:9792].rearrange("p (c t) -> p c t", c=C)
        decay = ra[:, 11264:13312].rearrange("p (c n) -> p c n", c=C)
        f1_gate = rd[:, 0:8192].rearrange("p (n c i) -> p n c i", n=4, c=C)
        f1_up = rd[:, 8192:16384].rearrange("p (n c i) -> p n c i", n=4, c=C)
        f1_wd = rd[:, 16384:17408].rearrange("p (c n) -> p c n", c=2)
        f1_swd = rd[:, 17408:19456].rearrange("p (c n) -> p c n", c=C)
        router = rd[:, 19456:19968].rearrange("p (c n) -> p c n", c=C)
        f1_sgate = ra[:, 13312:15360].rearrange("p (c n) -> p c n", c=C)
        f1_sup = ra[:, 15360:17408].rearrange("p (c n) -> p c n", c=C)
        f1_th = [ra[:, 512 * i:512 * i + 512] for i in range(2)]
        f1_a = ra[:, 1024:1536]
        f1_hs = ra[:, 1536:2048]
        f1_hsT = ra[:, 2048:2560].rearrange("p (c t) -> p c t", c=C)
        f1_b = ra[:, 2560:4608].rearrange("p (k i) -> p k i", k=8)
        f1_m = ra[:, 4608:4864]
        f1_mT = ra[:, 4864:5120].rearrange("p (c t) -> p c t", c=2)
        f1_e = ra[:, 5120:5248]
        f1_sel = ra[:, 5248:5376]
        f1_coef = ra[:, 5376:5504]
        f1_coefT = ra[:, 5504:5632]

        stats = sv[:, 0:6]
        mv = sv[:, 6:8]
        rstd = sv[:, 8:9]
        neghalf = sv[:, 9:10]
        var_eps = sv[:, 10:11]
        mx_x = sv[:, 12:28]
        rs_x = sv[:, 28:44]
        rr_x = sv[:, 44:60]
        asum = sv[:, 60:64]
        wscale = sv[:, 64:68]
        sc_qk = sv[:, 68:69]
        sc_vo = sv[:, 69:70]
        att_mx = [sv[:, 70:74], sv[:, 314:318]]
        att_rec = [sv[:, 74:78], sv[:, 318:322]]
        r_mx = sv[:, 78:79]
        top8 = sv[:, 79:87]
        r_sum = sv[:, 87:88]
        r_z = sv[:, 88:89]
        r_rec = sv[:, 89:90]
        top8f = sv[:, 90:98]
        r_e = sv[:, 98:130]
        r_rep = sv[:, 130:162]
        r_sel = sv[:, 162:194]
        r_em = sv[:, 194:226]
        coef = sv[:, 226:258]
        g_mean = sv[:, 258:274]
        g_var = sv[:, 274:290]
        g_nh = sv[:, 290:306]
        ck = sv[:, 306:314]
        mix = sb("mix", [P, 24])
        mix_p, mix_w = mix[:, 0:8], mix[:, 8:16]
        mix_s, mix_r = mix[:, 16:17], mix[:, 17:18]
        g_rstd = sb("g_rstd", [P, 16])

        ld_x, ld_const, ld_ctx, ld_kr, ld_b0, ld_c64 = map(sem, ("ld_x", "ld_const", "ld_ctx", "ld_kr", "ld_b0", "ld_c64"))
        ld_rope = sem("ld_rope")
        ld_a = [sem(f"ld_a{g}") for g in range(GROUPS)]
        ld_e0, ld_gw, ld_e1, ld_b1, ld_xpos, ld_decay = map(sem, ("ld_e0", "ld_gw", "ld_e1", "ld_b1", "ld_xpos", "ld_decay"))
        ld_gn, ld_amp, ld_esc = map(sem, ("ld_gn", "ld_amp", "ld_esc"))
        ld_ring = [sem(f"ld_ring{j}") for j in range(SLOTS)]
        ld_f1 = [sem(f"ld_f1_{n}") for n in range(8)]
        ld_f1s, ld_f1d, ld_router = map(sem, ("ld_f1s", "ld_f1d", "ld_router"))
        st_out = sem("st_out")
        dve_step, pool_step = sem("dve_step"), sem("pool_step")
        consts_ready, neghalf_ready = sem("consts_ready"), sem("neghalf_ready")
        var_ready, rstd_ready, xn_ready, xT_ps, xT_ready = map(sem, ("var_ready", "rstd_ready", "xn_ready", "xT_ps", "xT_ready"))
        rope_ready, rope_swap, c64T_ps, c64T_ready = map(sem, ("rope_ready", "rope_swap", "c64T_ps", "c64T_ready"))
        at_ps, at_sb, q_ps, q_sb, bw_ps, bw_sb, qk_ps, qk_sb, kvT_ps, kvT_sb = map(
            sem, ("at_ps", "at_sb", "q_ps", "q_sb", "bw_ps", "bw_sb", "qk_ps", "qk_sb", "kvT_ps", "kvT_sb"))
        s_ps, mx_done, exp_done, pt_ps, pt_sb0, pt_sb1, ctx_ps, ctx_sb, cT_ps, cT_sb, lat_ps, lat_sb, o_ps = map(
            sem, ("s_ps", "mx_done", "exp_done", "pt_ps", "pt_sb0", "pt_sb1", "ctx_ps", "ctx_sb", "cT_ps", "cT_sb", "lat_ps",
                  "lat_sb", "o_ps"))
        asum_done, sign_done, wsum_ps, wscale_done = map(sem, ("asum_done", "sign_done", "wsum_ps", "wscale_done"))
        aq_ps, aq_sb, akv_ps, ak_sb, av_sb, as_ps, asub, aexp, at2_ps, at2_sb, ao_ps, ao_sb, aoT_ps, aoT_sb, ap_ps = (
            [sem(f"{n}{i}") for i in range(2)] for n in
            ("aq_ps", "aq_sb", "akv_ps", "ak_sb", "av_sb", "as_ps", "asub", "aexp", "apt_ps", "apt_sb", "ao_ps", "ao_sb",
             "aoT_ps", "aoT_sb", "aproj_ps"))
        res_done = sem("res_done")
        r_ps, rmx_done, rexp_done, sel_done, pos_ps, coef_done = map(
            sem, ("r_ps", "rmx_done", "rexp_done", "sel_done", "pos_ps", "coef_done"))
        g_ps, u_ps, th_done, h_done, hT_ps, hT_sb, dn_done = map(
            sem, ("g_ps", "u_ps", "th_done", "h_done", "hT_ps", "hT_sb", "dn_done"))
        t_ps, rot_done, ret_v_sb, ret_th_done, ret_T_ps, ret_kT_sb, qbd_done, rs_ps, ret_pT_sb, y_ps, gvar_done, grstd_done = map(
            sem, ("t_ps", "rot_done", "ret_v_sb", "ret_th_done", "ret_T_ps", "ret_kT_sb", "qbd_done", "rs_ps", "ret_pT_sb", "y_ps",
                  "gvar_done", "grstd_done"))
        ret_o_done, ret_oT_ps, ret_oT_sb, proj_ps, ag_done = map(
            sem, ("ret_o_done", "ret_oT_ps", "ret_oT_sb", "proj_ps", "ag_done"))
        fr_ps, frmx, frexp, fcoef, fcT_ps, fcT_sb, fck_ps, mix_done = map(
            sem, ("fr_ps", "frmx", "frexp", "fcoef", "fcT_ps", "fcT_sb", "fck_ps", "mix_done"))
        fg_ps, fu_ps, fth, fh, fhT_ps, fhT_sb, fm_done, fmT_ps, fmT_sb, fo_ps, pool_m = map(
            sem, ("fg_ps", "fu_ps", "fth", "fh", "fhT_ps", "fhT_sb", "fm_done", "fmT_ps", "fmT_sb", "fo_ps", "pool_m"))

        block = stack.enter_context(nc.Block())

        @block.sync
        def _(sp):
            sp.dma_start(x[:, :], x_in).then_inc(ld_x, 16)
            sp.dma_start(cst[:, :], consts_d).then_inc(ld_const, 16)
            for g in range(GROUPS):
                sp.dma_start(ra[:, g * A_G:(g + 1) * A_G], wa_d[g]).then_inc(ld_a[g], 16)
                if g == 0:
                    sp.dma_start(rd[0:R0, 11264:13312], wkr_d).then_inc(ld_kr, 16)
                    sp.dma_start(rd[:, 0:2048], ctx_d).then_inc(ld_ctx, 16)
                    sp.dma_start(rd[:, 2048:4096], rope_d).then_inc(ld_rope, 16)
                    sp.dma_start(ctx64[:, :], ctx64_d).then_inc(ld_c64, 16)
            sp.dma_start(rb[:, :], wb_d).then_inc(ld_b0, 16)
            sp.dma_start(gatew[:, :, :], gatew_d.rearrange("p (c n) -> p c n", c=C)).then_inc(ld_gw, 16)
            sp.dma_start(xpos[:, :, :], xpos_d.rearrange("p (t n) -> p t n", t=2)).then_inc(ld_xpos, 16)
            sp.dma_start(gnwb[:, :, :], gn_d.rearrange("(a t) n -> a t n", a=1).broadcast_to([P, 2, D])).then_inc(ld_gn, 16)
            sp.dma_start(escale[:, :], escale_d.broadcast_to([P, P])).then_inc(ld_esc, 16)
            sp.dma_start(amp[:, :, :], amp_d).then_inc(ld_amp, 16)
            sp.wait_ge(qk_ps, GROUPS)
            sp.dma_start(we, e0_d).then_inc(ld_e0, 16)
            for j in range(3):
                sp.dma_start(slot[j], ring_d[j]).then_inc(ld_ring[j], 16)
            sp.wait_ge(ctx_ps, UNITS)
            sp.dma_start(slot[3], ring_d[3]).then_inc(ld_ring[3], 16)
            sp.wait_ge(res_done, 2)
            sp.dma_start(we, e1_d).then_inc(ld_e1, 16)
            sp.dma_start(ra[:, 13312:17408], f1s_d).then_inc(ld_f1s, 16)

            def refill(p, j):
                sp.wait_ge(dn_done, p - (SLOTS - 1))
                sp.dma_start(slot[j], ring_d[p]).then_inc(ld_ring[j], 16)

            for j in range(SLOTS):
                refill(SLOTS + j, j)
            sp.dma_start(rb[:, :], b1_d).then_inc(ld_b1, 16)
            for p in range(2 * SLOTS, PAIRS):
                refill(p, p % SLOTS)
            sp.wait_ge(dn_done, PAIRS)
            sp.dma_start(rd[:, 19456:19968], router_d).then_inc(ld_router, 16)
            for n in range(4):
                sp.dma_start(f1_gate[:, n], f1gu_d[n]).then_inc(ld_f1[n], 16)
                sp.dma_start(f1_up[:, n], f1gu_d[4 + n]).then_inc(ld_f1[4 + n], 16)
            sp.dma_start(rd[:, 16384:19456], f1d_d).then_inc(ld_f1d, 16)
            sp.wait_ge(res_done, 4)
            sp.dma_start(ra[:, 11264:13312], decay_d).then_inc(ld_decay, 16)
            sp.wait_ge(res_done, 6)
            sp.dma_start(out_d, x[:, :]).then_inc(st_out, 16)
            sp.wait_ge(st_out, 16)

        @block.gpsimd
        def _(pool):
            steps = [0]

            def link(ins):
                steps[0] += 1
                ins.then_inc(pool_step, 1)
                pool.wait_ge(pool_step, steps[0])

            pool.memset(ones[:, :], 1.0).then_inc(consts_ready, 1)
            link(pool.memset(neghalf, -0.5))
            pool.memset(g_nh, -0.5).then_inc(consts_ready, 1)

            def rstd_of(i):
                pool.wait_ge(var_ready, i + 1)
                link(pool.tensor_scalar(var_eps, mv[:, 1:2], EPS, None, ALU.add))
                pool.tensor_tensor(rstd, var_eps, neghalf, ALU.pow).then_inc(rstd_ready, 1)

            rstd_of(0)
            pool.wait_ge(ld_ctx, 16)
            pool.wait_ge(ld_rope, 16)
            for b in range(B):
                if b:
                    pool.wait_ge(rope_ready, b)
                pool.tensor_tensor(rope_tmp[:, :, 0:64], ctxr[:, b, :, 64:128], rope_sin[:, :, 0:64], ALU.mult)
                pool.tensor_tensor(rope_tmp[:, :, 64:128], ctxr[:, b, :, 0:64], rope_sin[:, :, 64:128],
                                   ALU.mult).then_inc(rope_swap, 1)
            for i in range(1, 5):
                rstd_of(i)
            pool.wait_ge(gvar_done, 1)
            pool.wait_ge(consts_ready, 2)
            pool.tensor_tensor(g_rstd[:, :], g_var, g_nh, ALU.pow).then_inc(grstd_done, 1)
            rstd_of(5)
            pool.wait_ge(fh, 2)
            link(pool.tensor_tensor(f1_m, f1_b[:, 0, :], f1_b[:, 1, :], ALU.add))
            for n in range(1, 4):
                pool.wait_ge(fh, n + 2)
                for k in (2 * n, 2 * n + 1):
                    if k < 7:
                        link(pool.tensor_tensor(f1_m, f1_m, f1_b[:, k, :], ALU.add))
            pool.tensor_tensor(f1_m, f1_m, f1_b[:, 7, :], ALU.add).then_inc(fm_done, 1)

        @block.scalar
        def _(act):
            act.wait_ge(ld_c64, 16)

            def kvT_copy(g):
                act.wait_ge(kvT_ps, g + 1)
                dst = kvT[:, g // 2, (g % 2) * 512:(g % 2) * 512 + 512]
                act.activation(dst, ps[:, 7, :], ACT.Copy).then_inc(kvT_sb, 1)

            for g in range(GROUPS):
                act.wait_ge(q_ps, g + 1)
                act.activation(qT_x[:, 4 * g:4 * g + 4, :].rearrange("p h t -> p (h t)"), ps[:, g % 2, :],
                               ACT.Copy).then_inc(q_sb, 1)
                kvT_copy(g)

            def exp_unit(u):
                act.wait_ge(mx_done, u + 1)
                if u >= 2:
                    act.wait_ge(pt_ps, 2 * (u - 1))
                act.activation(prob_x[u % 2].rearrange("p j l -> p (j l)"),
                               ps[:, 2 * (u % 2):2 * (u % 2) + 2, :].rearrange("p a n -> p (a n)"), ACT.Exp,
                               bias=mx_x[:, u:u + 1], accum_out=rs_x[:, u:u + 1]).then_inc(exp_done, 1)

            def probT_copy(u):
                act.wait_ge(pt_ps, 2 * u + 1)
                if u >= 2:
                    act.wait_ge(ctx_ps, u - 1)
                act.activation(probT_x[u % 2][:, 0:4, :].rearrange("p j r -> p (j r)"), ps[:, 4, :],
                               ACT.Copy).then_inc(pt_sb0, 1)

            def ctxT_copy(u):
                act.wait_ge(cT_ps, u + 1)
                act.activation(ctxT[:, 2 * (u // 2):2 * (u // 2) + 2, u % 2, :],
                               ps[:, 7, 0:P].rearrange("p (h s) -> p h s", h=2), ACT.Copy).then_inc(cT_sb, 1)

            for i in range(UNITS + 3):
                if i < UNITS:
                    exp_unit(i)
                if 1 <= i <= UNITS:
                    probT_copy(i - 1)
                if i >= 3:
                    ctxT_copy(i - 3)
                if i == 12:
                    act.wait_ge(asum_done, 4)
                    act.activation(we, we, ACT.Sign).then_inc(sign_done, 1)
            for g in range(0, GROUPS, 2):
                act.wait_ge(lat_ps, g + 1)
                act.activation(latT[:, 4 * g:4 * g + 4, :].rearrange("p h t -> p (h t)"), ps[:, g, :],
                               ACT.Copy).then_inc(lat_sb, 1)

            def attention(a):
                n = att_banks[a]
                act.wait_ge(aq_ps[a], 1)
                act.activation(att_qT[a].rearrange("p i t -> p (i t)"), ps[:, 0, :], ACT.Copy).then_inc(aq_sb[a], 1)
                if a == 0:
                    act.wait_ge(wscale_done, 1)
                for i in range(n + 1):
                    if i < n:
                        act.wait_ge(asub[a], i + 1)
                        p = att_prob[a][:, i].rearrange("p h t -> p (h t)")
                        act.activation(p, p, ACT.Exp, scale=sc_qk if a == 0 else att_hd[a] ** -0.5).then_inc(aexp[a], 1)
                    if i >= 1:
                        act.wait_ge(at2_ps[a], i)
                        act.activation(att_probT[a][:, i - 1].rearrange("p h t -> p (h t)"), ps[:, 5 + (i - 1) % 2, :],
                                       ACT.Copy).then_inc(at2_sb[a], 1)

            attention(0)

            act.wait_ge(rmx_done, 1)
            act.activation(r_e, ps[:, 0, 0:E0], ACT.Exp, bias=r_mx).then_inc(rexp_done, 1)

            def moe_tanh(p, k, first=False):
                act.wait_ge(g_ps, p + 1)
                if not first:
                    act.wait_ge(h_done, p - 1)
                act.activation(moe_th[k], ps[:, 2 + k, 0:384], ACT.Tanh, scale=0.5).then_inc(th_done, 1)

            def moe_hT_copy(p, k, first=False):
                act.wait_ge(hT_ps, p + 1)
                if not first:
                    act.wait_ge(dn_done, p - 1)
                act.activation(moe_hT[k].rearrange("p c t -> p (c t)"), ps[:, 6, 0:384], ACT.Copy).then_inc(hT_sb, 1)

            for p in range(PAIRS):
                moe_tanh(p, p % 2, p < 2)
                if p:
                    moe_hT_copy(p - 1, (p - 1) % 2, p < 3)
            moe_hT_copy(PAIRS - 1, 1)

            attention(1)

            act.wait_ge(t_ps, 3)
            act.activation(ret_v[:, 0:512], ps[:, 2, :], ACT.Copy).then_inc(ret_v_sb, 1)
            act.wait_ge(t_ps, 4)
            act.activation(ret_th, ps[:, 3, :], ACT.Tanh, scale=0.5).then_inc(ret_th_done, 1)
            act.wait_ge(ret_T_ps, 2)
            act.activation(ret_kT.rearrange("p c t -> p (c t)"), ps[:, 5, :], ACT.Copy).then_inc(ret_kT_sb, 1)

            def f1_tanh(n):
                act.wait_ge(fg_ps, n + 1)
                if n >= 2:
                    act.wait_ge(fh, n - 1)
                act.activation(f1_th[n % 2], ps[:, 1 + n % 2, :], ACT.Tanh, scale=0.5).then_inc(fth, 1)

            act.wait_ge(frmx, 1)
            act.activation(f1_e, ps[:, 0, 0:P], ACT.Exp, bias=r_mx, accum_out=r_z).then_inc(frexp, 1)
            f1_tanh(0)
            f1_tanh(1)
            act.wait_ge(fhT_ps, 1)
            act.activation(f1_hsT.rearrange("p c t -> p (c t)"), ps[:, 5, :], ACT.Copy).then_inc(fhT_sb, 1)
            for n in range(2, 5):
                f1_tanh(n)
            act.wait_ge(fmT_ps, 1)
            act.activation(f1_mT.rearrange("p c t -> p (c t)"), ps[:, 6, 0:256], ACT.Copy).then_inc(fmT_sb, 1)

        @block.vector
        def _(dve):
            steps = [0]

            def link(ins):
                steps[0] += 1
                ins.then_inc(dve_step, 1)
                dve.wait_ge(dve_step, steps[0])

            def layernorm(i):
                link(dve.bn_stats(stats, x[:, :]))
                dve.bn_aggr(mv, stats).then_inc(var_ready, 1)
                dve.wait_ge(rstd_ready, i + 1)
                dve.tensor_scalar(xn[:, :], x[:, :], mv[:, 0:1], rstd, ALU.subtract, ALU.mult).then_inc(xn_ready, 1)

            def xT_copy(i):
                dve.wait_ge(xT_ps, i + 1)
                dve.tensor_copy(xnT[:, :, :].rearrange("p c t -> p (c t)"), ps[:, 7, :]).then_inc(xT_ready, 1)

            def add_residual(psum, scale=None):
                if scale is None:
                    dve.tensor_tensor(x[:, :], psum, x[:, :], ALU.add).then_inc(res_done, 1)
                else:
                    dve.scalar_tensor_tensor(x[:, :], psum, scale, x[:, :], ALU.mult, ALU.add).then_inc(res_done, 1)
                residuals[0] += 1
                dve.wait_ge(res_done, residuals[0])

            residuals = [0]
            dve.wait_ge(ld_x, 16)
            layernorm(0)
            dve.wait_ge(ld_const, 16)
            dve.tensor_copy(identb[:, :], ident)
            dve.tensor_copy(maskb[:, :, :], maskf.unsqueeze(1).broadcast_to([P, 4, P])).then_inc(consts_ready, 1)
            xT_copy(0)

            def rope(b):
                link(dve.tensor_tensor(kvr[:, b], ctxr[:, b], rope_cos, ALU.mult))
                dve.wait_ge(rope_swap, b + 1)
                dve.tensor_tensor(kvr[:, b], kvr[:, b], rope_tmp, ALU.add).then_inc(rope_ready, 1)

            def at_copy(g):
                dve.wait_ge(at_ps, g + 1)
                dve.tensor_copy(qrk[0:R0, 4 * g:4 * g + 4, :].rearrange("p h t -> p (h t)"),
                                ps[0:R0, 2 + g % 2, :]).then_inc(at_sb, 1)

            def bw_copy(g):
                dve.wait_ge(bw_ps, g + 1)
                dve.tensor_copy(qkw[:, 4 * g:4 * g + 4, :].rearrange("p h t -> p (h t)"), ps[:, 4 + g % 2, :]).then_inc(bw_sb, 1)

            def qk_copy(g):
                dve.wait_ge(qk_ps, g + 1)
                src = ps[:, 6, :].rearrange("p (h b s) -> p h b s", h=4, b=B)
                for b in range(B):
                    ins = dve.tensor_copy(qk_x[:, b, 4 * g:4 * g + 4, :], src[:, :, b, :])
                ins.then_inc(qk_sb, 1)

            at_copy(0)
            dve.wait_ge(ld_ctx, 16)
            dve.wait_ge(ld_rope, 16)
            rope(0)
            rope(1)
            bw_copy(0)
            for g in range(1, GROUPS):
                at_copy(g)
                qk_copy(g - 1)
                bw_copy(g)
            qk_copy(GROUPS - 1)
            dve.wait_ge(c64T_ps, 1)
            dve.tensor_copy(ctx64T[:, :], ps[:, 7, 0:P]).then_inc(c64T_ready, 1)

            def row_max(u):
                dve.wait_ge(s_ps, u + 1)
                dve.tensor_reduce(mx_x[:, u:u + 1], ps[:, 2 * (u % 2):2 * (u % 2) + 2, :].rearrange("p a n -> p (a n)"),
                                  AX.X, ALU.max, negate=True).then_inc(mx_done, 1)

            def probT_copy(u):
                dve.wait_ge(pt_ps, 2 * u + 2)
                if u >= 2:
                    dve.wait_ge(ctx_ps, u - 1)
                dve.tensor_copy(probT_x[u % 2][:, 4:8, :].rearrange("p j r -> p (j r)"), ps[:, 5, :]).then_inc(pt_sb1, 1)

            def ctx_scale(u):
                dve.wait_ge(exp_done, u + 1)
                link(dve.reciprocal(rr_x[:, u:u + 1], rs_x[:, u:u + 1]))
                dve.wait_ge(ctx_ps, u + 1)
                if u >= 1:
                    dve.wait_ge(cT_ps, u)
                dve.tensor_scalar(xn[:, 0:P], ps[:, 6, 0:P], rr_x[:, u:u + 1], None, ALU.mult).then_inc(ctx_sb, 1)

            parts = [(0, 2048), (2048, 2560), (2560, 3072), (3072, 5120)]
            for i in range(UNITS + 2):
                if i < UNITS:
                    row_max(i)
                if 1 <= i <= UNITS:
                    probT_copy(i - 1)
                if i >= 2:
                    ctx_scale(i - 2)
                if 8 <= i < 12:
                    if i == 8:
                        dve.wait_ge(ld_e0, 16)
                    a0, a1 = parts[i - 8]
                    dve.tensor_reduce(asum[:, i - 8:i - 7], we[:, a0:a1], AX.X, ALU.add,
                                      apply_absolute_value=True).then_inc(asum_done, 1)
            for g in range(1, GROUPS, 2):
                dve.wait_ge(lat_ps, g + 1)
                dve.tensor_copy(latT[:, 4 * g:4 * g + 4, :].rearrange("p h t -> p (h t)"), ps[:, g, :]).then_inc(lat_sb, 1)
            dve.wait_ge(wsum_ps, 1)
            for m, n in enumerate((D * D, P * D, P * D, D * D)):
                ins = dve.tensor_scalar(wscale[:, m:m + 1], ps[:, 5, m:m + 1], 1.0 / n, EPS, ALU.mult, ALU.max)
            link(ins)
            dve.scalar_tensor_tensor(sc_qk, wscale[:, 0:1], att_hd[0] ** -0.5, wscale[:, 1:2], ALU.mult, ALU.mult)
            dve.tensor_tensor(sc_vo, wscale[:, 2:3], wscale[:, 3:4], ALU.mult).then_inc(wscale_done, 1)
            dve.wait_ge(o_ps, 1)
            add_residual(ps[:, 4, :])

            def attention(a):
                n, hd, heads = att_banks[a], att_hd[a], att_kbd[a].shape[1]
                vw = att_v[a][:, 0:(heads) * (hd + 1)].rearrange("p (h e) -> p h e", e=hd + 1)

                def make_k():
                    dve.wait_ge(akv_ps[a], 1)
                    if a == 0:
                        ins = dve.tensor_tensor(att_kbd[0], ps[:, 1, 0:P].unsqueeze(1).broadcast_to([P, 8, P]),
                                                m16.unsqueeze(2).broadcast_to([P, 8, P]), ALU.mult)
                    else:
                        for c in range(4):
                            ins = dve.tensor_tensor(att_kbd[1][:, 4 * c:4 * c + 4],
                                                    ps[:, 1, c * P:(c + 1) * P].unsqueeze(1).broadcast_to([P, 4, P]),
                                                    m32.unsqueeze(2).broadcast_to([P, 4, P]), ALU.mult)
                    ins.then_inc(ak_sb[a], 1)

                def make_v():
                    link(dve.memset(att_v[a], 1.0))
                    dve.wait_ge(akv_ps[a], 2)
                    dve.tensor_copy(vw[:, :, 0:hd], ps[:, 2, 0:heads * hd].rearrange("p (h d) -> p h d", d=hd)).then_inc(av_sb[a], 1)

                if a == 1:
                    make_k()
                    make_v()
                layernorm(1 if a == 0 else 3)
                xT_copy(1 if a == 0 else 3)
                if a == 0:
                    make_k()
                    make_v()
                if a == 0:
                    o4 = att_o[0].rearrange("p (k g d) -> p g k d", k=8, g=4)
                    outs = [o4[:, i // 2, 4 * (i % 2):4 * (i % 2) + 4, :] for i in range(8)]
                else:
                    o4 = att_o[1].rearrange("p (i h d) -> p i h d", i=4, h=4)
                    outs = [o4[:, i] for i in range(4)]
                for i in range(n + 2):
                    if i < n:
                        dve.wait_ge(as_ps[a], i + 1)
                        s = ps[:, 3 + i % 2, :].rearrange("p (h t) -> p h t", h=4)
                        mx = att_mx[i % 2]
                        link(dve.tensor_reduce(mx, s, AX.X, ALU.max))
                        dve.tensor_tensor(att_prob[a][:, i], s, mx.unsqueeze(2).broadcast_to([P, 4, P]),
                                          ALU.subtract).then_inc(asub[a], 1)
                    if i >= 2:
                        dve.wait_ge(ao_ps[a], i - 1)
                        o = ps[:, 7 if i % 2 == 0 else 0, :].rearrange("p (h t) -> p h t", h=4)
                        rec = att_rec[i % 2]
                        link(dve.reciprocal(rec, o[:, :, hd]))
                        dve.tensor_tensor(outs[i - 2], o[:, :, 0:hd], rec.unsqueeze(2).broadcast_to([P, 4, hd]),
                                          ALU.mult).then_inc(ao_sb[a], 1)
                dve.wait_ge(aoT_ps[a], 1)
                dve.tensor_copy(att_oT[a].rearrange("p c t -> p (c t)"), ps[:, 1, :]).then_inc(aoT_sb[a], 1)
                dve.wait_ge(ap_ps[a], 1)
                add_residual(ps[:, 2, :], sc_vo if a == 0 else None)

            attention(0)

            layernorm(2)
            xT_copy(2)
            dve.wait_ge(r_ps, 1)
            dve.tensor_reduce(r_mx, ps[:, 0, 0:E0], AX.X, ALU.max, negate=True).then_inc(rmx_done, 1)
            dve.wait_ge(rexp_done, 1)
            link(dve.max(top8, r_e))
            link(dve.match_replace(r_rep, top8, r_e, -1.0))
            dve.tensor_tensor(r_sel, r_rep, r_e, ALU.not_equal).then_inc(sel_done, 1)
            link(dve.tensor_reduce(r_sum, top8, AX.X, ALU.add))
            link(dve.reciprocal(r_rec, r_sum))
            dve.wait_ge(sel_done, 1)
            link(dve.tensor_tensor(r_em, r_e, r_sel, ALU.mult))
            dve.wait_ge(pos_ps, 1)
            link(dve.scalar_tensor_tensor(r_em, ps[:, 1, 0:E0], float(CAP), r_em, ALU.is_lt, ALU.mult))
            link(dve.tensor_scalar(coef, r_em, r_rec, 0.5, ALU.mult, ALU.mult))

            def moe_hidden(p, k, first=False):
                dve.wait_ge(th_done, p + 1)
                link(dve.scalar_tensor_tensor(moe_a, moe_th[k], 1.0, ps[:, 2 + k, 0:384], ALU.add, ALU.mult))
                dve.wait_ge(u_ps, p + 1)
                if not first:
                    dve.wait_ge(hT_ps, p - 1)
                for e in range(2):
                    ins = dve.scalar_tensor_tensor(moe_h[k][:, e * I0:(e + 1) * I0], moe_a[:, e * I0:(e + 1) * I0],
                                                   coef[:, 2 * p + e:2 * p + e + 1],
                                                   ps[:, 4 + k, e * I0:(e + 1) * I0], ALU.mult, ALU.mult)
                ins.then_inc(h_done, 1)
                dve.wait_ge(h_done, p + 1)

            for p in range(PAIRS):
                moe_hidden(p, p % 2, p < 2)
            dve.wait_ge(dn_done, PAIRS)
            add_residual(ps[:, 7, :])

            attention(1)

            layernorm(4)
            xT_copy(4)
            dve.wait_ge(t_ps, 2)
            dve.wait_ge(ld_xpos, 16)
            qk = ps[:, 0:2, :]
            pairs_in = qk.rearrange("p t (n two) -> p t n two", two=2)
            pairs_tmp = rot_tmp.rearrange("p t (n two) -> p t n two", two=2)
            sin2 = xpos[:, 1, :].rearrange("p (n two) -> p n two", two=2)
            dve.tensor_tensor(rot, qk, xpos[:, 0:1, :].broadcast_to([P, 2, D]), ALU.mult)
            for k in range(2):
                ins = dve.tensor_tensor(pairs_tmp[:, :, :, k], pairs_in[:, :, :, 1 - k],
                                        sin2[:, :, k].unsqueeze(1).broadcast_to([P, 2, D // 2]), ALU.mult)
            link(ins)
            for t in range(2):
                dve.tensor_tensor(rot[:, t], rot[:, t], rot_tmp[:, t], ALU.add).then_inc(rot_done, 1)
            dve.wait_ge(ret_th_done, 1)
            dve.scalar_tensor_tensor(ret_ag, ret_th, 1.0, ps[:, 3, :], ALU.add, ALU.mult).then_inc(ag_done, 1)
            dve.wait_ge(ret_T_ps, 1)
            for c in range(C):
                dve.tensor_tensor(ret_qbd[:, c], ps[:, 4, c * P:(c + 1) * P].unsqueeze(1).broadcast_to([P, 4, P]),
                                  m32.unsqueeze(2).broadcast_to([P, 4, P]), ALU.mult).then_inc(qbd_done, 1)
            dve.wait_ge(ld_decay, 16)
            for c in range(C):
                dve.wait_ge(rs_ps, c + 1)
                dve.tensor_tensor(ret_pT[:, c].rearrange("p h t -> p (h t)"), ps[:, (6, 7, 0, 1)[c], :], decay[:, c, :],
                                  ALU.mult).then_inc(ret_pT_sb, 1)
            for c in range(C):
                dve.wait_ge(y_ps, c + 1)
                ins = dve.tensor_copy(ret_y[:, 4 * c:4 * c + 4, :],
                                      ps[:, 4 + c, :].rearrange("p (h t) -> p h t", h=4)[:, :, 0:32])
            link(ins)
            link(dve.tensor_reduce(g_mean, ret_y, AX.X, ALU.add))
            link(dve.tensor_scalar(g_mean, g_mean, 1.0 / 32, None, ALU.mult))
            link(dve.tensor_tensor(ret_y, ret_y, g_mean.unsqueeze(2).broadcast_to([P, 16, 32]), ALU.subtract))
            link(dve.tensor_tensor(ret_sq, ret_y, ret_y, ALU.mult))
            link(dve.tensor_reduce(g_var, ret_sq, AX.X, ALU.add))
            dve.tensor_scalar(g_var, g_var, 1.0 / 32, EPS, ALU.mult, ALU.add).then_inc(gvar_done, 1)
            dve.wait_ge(grstd_done, 1)
            link(dve.tensor_tensor(ret_y, ret_y, g_rstd[:, :].unsqueeze(2).broadcast_to([P, 16, 32]), ALU.mult))
            dve.wait_ge(ld_gn, 16)
            yf = ret_y.rearrange("p h d -> p (h d)")
            link(dve.tensor_tensor(yf, yf, gnwb[:, 0, :], ALU.mult))
            link(dve.tensor_tensor(yf, yf, gnwb[:, 1, :], ALU.add))
            dve.scalar_tensor_tensor(yf, yf, 0.5, ret_ag, ALU.mult, ALU.mult).then_inc(ret_o_done, 1)
            dve.wait_ge(ret_oT_ps, 1)
            dve.tensor_copy(ret_oT.rearrange("p c t -> p (c t)"), ps[:, 0, :]).then_inc(ret_oT_sb, 1)
            dve.wait_ge(ld_amp, 16)
            link(dve.tensor_tensor(amp[:, :, :], amp[:, :, :], amp[:, :, :], ALU.mult))
            link(dve.tensor_tensor(mix_p, amp[:, :, 0], amp[:, :, 1], ALU.add))
            link(dve.tensor_reduce(mix_s, mix_p, AX.X, ALU.add))
            link(dve.tensor_scalar(mix_s, mix_s, 1e-8, None, ALU.add))
            link(dve.reciprocal(mix_r, mix_s))
            dve.tensor_scalar(mix_w, mix_p, mix_r, None, ALU.mult).then_inc(mix_done, 1)
            dve.wait_ge(proj_ps, 1)
            add_residual(ps[:, 1, :])

            layernorm(5)
            xT_copy(5)
            dve.wait_ge(fr_ps, 1)
            dve.tensor_reduce(r_mx, ps[:, 0, 0:P], AX.X, ALU.max, negate=True).then_inc(frmx, 1)
            dve.wait_ge(frexp, 1)
            link(dve.max(top8, f1_e))
            link(dve.max_index(top8i[:, :], top8, f1_e))
            link(dve.tensor_copy(top8f, top8i[:, :]))
            link(dve.tensor_scalar(f1_sel, iota, top8f[:, 0:1], None, ALU.is_equal))
            for k in range(1, 4):
                link(dve.scalar_tensor_tensor(f1_sel, iota, top8f[:, k:k + 1], f1_sel, ALU.is_equal, ALU.add))
            link(dve.tensor_reduce(r_sum, top8[:, 0:4], AX.X, ALU.add))
            link(dve.scalar_tensor_tensor(r_sum, r_z, 1e-8, r_sum, ALU.mult, ALU.add))
            link(dve.reciprocal(r_rec, r_sum))
            link(dve.tensor_tensor(f1_sel, f1_sel, f1_e, ALU.mult))
            dve.wait_ge(ld_esc, 16)
            dve.scalar_tensor_tensor(f1_coef, f1_sel, r_rec, escale[:, :], ALU.mult, ALU.mult).then_inc(fcoef, 1)

            def f1_gated(n):
                dve.wait_ge(fth, n + 1)
                link(dve.scalar_tensor_tensor(f1_a, f1_th[n % 2], 1.0, ps[:, 1 + n % 2, :], ALU.add, ALU.mult))
                dve.wait_ge(fu_ps, n + 1)

            f1_gated(0)
            dve.scalar_tensor_tensor(f1_hs, f1_a, 0.5, ps[:, 3, :], ALU.mult, ALU.mult).then_inc(fh, 1)
            dve.wait_ge(fh, 1)
            dve.wait_ge(fcT_ps, 1)
            dve.tensor_copy(f1_coefT, ps[:, 0, 0:P]).then_inc(fcT_sb, 1)
            dve.wait_ge(fck_ps, 1)
            link(dve.tensor_scalar(ck, ps[:, 0, 0:8], 0.5, None, ALU.mult))
            for n in range(1, 5):
                f1_gated(n)
                for k in range(2):
                    kk = 2 * (n - 1) + k
                    ins = dve.scalar_tensor_tensor(f1_b[:, kk, :], f1_a[:, 256 * k:256 * k + 256], ck[:, kk:kk + 1],
                                                   ps[:, 3 + n % 2, 256 * k:256 * k + 256], ALU.mult, ALU.mult)
                ins.then_inc(fh, 1)
                dve.wait_ge(fh, n + 1)
            dve.wait_ge(fo_ps, 1)
            add_residual(ps[:, 7, :])

        @block.tensor
        def _(pe):
            def x_transposes(i):
                pe.wait_ge(xn_ready, i + 1)
                src = xn[:, :].rearrange("p (q c) -> p c q", c=C)
                for c in range(C):
                    ins = pe.transpose(ps[:, 7, c * P:(c + 1) * P], src[:, c, :], ident)
                ins.then_inc(xT_ps, 1)

            def qrk_products(g):
                pe.wait_ge(ld_a[g], 16)
                if g >= 2:
                    pe.wait_ge(at_sb, g - 1)
                for h in range(4):
                    for c in range(KQ):
                        ins = pe.matmul(ps[0:R0, 2 + g % 2, h * P:(h + 1) * P], wqr(g)[:, h, c, :], wkcq(g)[:, h, c, :],
                                        start=(c == 0), stop=(c == KQ - 1))
                ins.then_inc(at_ps, 1)

            def queries(g):
                if g >= 2:
                    pe.wait_ge(q_sb, g - 1)
                for h in range(4):
                    for c in range(C):
                        ins = pe.matmul(ps[:, g % 2, h * P:(h + 1) * P], wq_x(g)[:, c, h * P:(h + 1) * P], xnT[:, c, :],
                                        start=(c == 0), stop=(c == C - 1))
                ins.then_inc(q_ps, 1)

            def context_transposes(g):
                if g == 0:
                    pe.wait_ge(xT_ready, 1)
                    pe.wait_ge(rope_ready, 1)
                else:
                    pe.wait_ge(kvT_sb, g)
                if g == 2:
                    pe.wait_ge(rope_ready, 2)
                for j in range(4):
                    ins = pe.transpose(ps[:, 7, j * P:(j + 1) * P], kvr[:, g // 2, 4 * (g % 2) + j, :], ident)
                ins.then_inc(kvT_ps, 1)

            def qkw_products(g):
                pe.wait_ge(at_sb, g + 1)
                if g == 0:
                    pe.wait_ge(ld_kr, 16)
                if g >= 2:
                    pe.wait_ge(bw_sb, g - 1)
                for h in range(4):
                    ins = pe.matmul(ps[:, 4 + g % 2, h * P:(h + 1) * P], qrk[0:R0, 4 * g + h, :], wkrT[0:R0, 4 * g + h, :],
                                    start=True, stop=True)
                ins.then_inc(bw_ps, 1)

            def latent_queries(g):
                pe.wait_ge(bw_sb, g + 1)
                pe.wait_ge(q_sb, g + 1)
                if g:
                    pe.wait_ge(qk_sb, g)
                for h in range(4):
                    ins = pe.matmul(ps[:, 6, h * P:(h + 1) * P], qkw[:, 4 * g + h, :], qT_x[:, 4 * g + h, :],
                                    start=True, stop=True)
                ins.then_inc(qk_ps, 1)

            pe.wait_ge(ld_const, 16)
            x_transposes(0)
            qrk_products(0)
            pe.wait_ge(xT_ready, 1)
            for g in range(GROUPS):
                if g:
                    qrk_products(g)
                queries(g)
                context_transposes(g)
                if g:
                    latent_queries(g - 1)
                qkw_products(g)
            latent_queries(GROUPS - 1)
            pe.wait_ge(kvT_sb, GROUPS)
            pe.wait_ge(ld_c64, 16)
            pe.transpose(ps[:, 7, 0:P], ctx64[:, :], ident).then_inc(c64T_ps, 1)

            def scores(u):
                if u == 0:
                    pe.wait_ge(qk_sb, GROUPS)
                if u >= 2:
                    pe.wait_ge(exp_done, u - 1)
                rows = qk_x[:, u % 2, 2 * (u // 2):2 * (u // 2) + 2, :].rearrange("p h s -> p (h s)")
                for half in range(2):
                    ins = pe.matmul(ps[:, 2 * (u % 2) + half, :], rows, kvT[:, u % 2, half * 512:half * 512 + 512],
                                    start=True, stop=True)
                ins.then_inc(s_ps, 1)

            def prob_transposes(u):
                pe.wait_ge(exp_done, u + 1)
                for half in range(2):
                    if u:
                        pe.wait_ge((pt_sb0, pt_sb1)[half], u)
                    for j in range(4):
                        ins = pe.transpose(ps[:, 4 + half, j * P:(j + 1) * P], prob_x[u % 2][:, 4 * half + j, :], ident)
                    ins.then_inc(pt_ps, 1)

            def context_products(u):
                pe.wait_ge(pt_sb0, u + 1)
                pe.wait_ge(pt_sb1, u + 1)
                if u:
                    pe.wait_ge(ctx_sb, u)
                for j in range(J):
                    ins = pe.matmul(ps[:, 6, 0:P], probT_x[u % 2][:, j, :], kvr[:, u % 2, j, :], start=(j == 0), stop=(j == J - 1))
                ins.then_inc(ctx_ps, 1)

            def result_transpose(u):
                pe.wait_ge(ctx_sb, u + 1)
                if u == 0:
                    pe.wait_ge(c64T_ready, 1)
                else:
                    pe.wait_ge(cT_sb, u)
                pe.transpose(ps[:, 7, 0:P], xn[:, 0:P], ident).then_inc(cT_ps, 1)

            for i in range(UNITS + 3):
                if i < UNITS:
                    scores(i)
                if i >= 3:
                    result_transpose(i - 3)
                if 2 <= i < UNITS + 2:
                    context_products(i - 2)
                if 1 <= i <= UNITS:
                    prob_transposes(i - 1)
            pe.wait_ge(cT_sb, UNITS)
            pe.wait_ge(ld_b0, 16)
            for g in range(GROUPS):
                for h in range(4 * g, 4 * g + 4):
                    ins = pe.matmul(ps[:, g, (h % 4) * P:(h % 4 + 1) * P], wkv_x[:, h, :],
                                    ctxT[:, h].rearrange("p b s -> p (b s)"), start=True, stop=True)
                ins.then_inc(lat_ps, 1)
            pe.wait_ge(asum_done, 4)
            pe.wait_ge(consts_ready, 3)
            pe.matmul(ps[:, 5, 0:4], ones[:, :], asum, start=True, stop=True).then_inc(wsum_ps, 1)
            pe.wait_ge(lat_sb, GROUPS)
            for h in range(H0):
                ins = pe.matmul(ps[:, 4, :], latT[:, h, :], wo_x[:, h, :], start=(h == 0), stop=(h == H0 - 1))
            ins.then_inc(o_ps, 1)

            def attention(a):
                n, hd = att_banks[a], att_hd[a]
                ln = 1 if a == 0 else 3

                def keys_values():
                    if a == 0:
                        for c in range(C):
                            ins = pe.matmul(ps[:, 1, 0:P], e_wk0[:, c, :], xnT[:, c, :], start=(c == 0), stop=(c == C - 1))
                        ins.then_inc(akv_ps[a], 1)
                        for c in range(C):
                            ins = pe.matmul(ps[:, 2, 0:P], xnT[:, c, :], e_wv0[:, c, :], start=(c == 0), stop=(c == C - 1))
                        ins.then_inc(akv_ps[a], 1)
                    else:
                        pe.wait_ge(res_done, 3)
                        for c in range(4):
                            ins = pe.matmul(ps[:, 1, c * P:(c + 1) * P], e_wk1[:, c * P:(c + 1) * P], ctx64T[:, :],
                                            start=True, stop=True)
                        ins.then_inc(akv_ps[a], 1)
                        pe.matmul(ps[:, 2, :], ctx64T[:, :], e_wv1, start=True, stop=True).then_inc(akv_ps[a], 1)

                if a == 0:
                    pe.wait_ge(sign_done, 1)
                else:
                    pe.wait_ge(ld_e1, 16)
                    keys_values()
                x_transposes(ln)
                pe.wait_ge(xT_ready, ln + 1)
                for g in range(4):
                    for c in range(C):
                        ins = pe.matmul(ps[:, 0, g * P:(g + 1) * P], e_wq[:, c, g * P:(g + 1) * P], xnT[:, c, :],
                                        start=(c == 0), stop=(c == C - 1))
                ins.then_inc(aq_ps[a], 1)
                if a == 0:
                    keys_values()
                pe.wait_ge(consts_ready, 3)
                for i in range(n + 2):
                    if i < n:
                        if i == 0:
                            pe.wait_ge(aq_sb[a], 1)
                            pe.wait_ge(ak_sb[a], 1)
                        if i >= 2:
                            pe.wait_ge(asub[a], i - 1)
                        if a == 0:
                            q, k = att_qT[0][:, i // 2, :], att_kbd[0][:, 4 * (i % 2):4 * (i % 2) + 4]
                        else:
                            q, k = att_qT[1][:, i, :], att_kbd[1][:, 4 * i:4 * i + 4]
                        pe.matmul(ps[:, 3 + i % 2, :], q, k.rearrange("p h t -> p (h t)"), start=True, stop=False)
                        pe.matmul(ps[:, 3 + i % 2, :], identb[:, :], maskb[:, :, :].rearrange("p h t -> p (h t)"),
                                  start=False, stop=True).then_inc(as_ps[a], 1)
                    if i >= 2:
                        m = i - 2
                        pe.wait_ge(at2_sb[a], m + 1)
                        if m == 0:
                            pe.wait_ge(av_sb[a], 1)
                        if m >= 2:
                            pe.wait_ge(ao_sb[a], m - 1)
                        for hh in range(4):
                            v0 = (4 * (m % 2) + hh if a == 0 else 4 * m + hh) * (hd + 1)
                            ins = pe.matmul(ps[:, 7 if m % 2 == 0 else 0, hh * P:hh * P + 97], att_probT[a][:, m, hh, :],
                                            att_v[a][:, v0:v0 + 97], start=True, stop=True)
                        ins.then_inc(ao_ps[a], 1)
                    if 1 <= i <= n:
                        pe.wait_ge(aexp[a], i)
                        if i >= 3:
                            pe.wait_ge(at2_sb[a], i - 2)
                        for hh in range(4):
                            ins = pe.transpose(ps[:, 5 + (i - 1) % 2, hh * P:(hh + 1) * P], att_prob[a][:, i - 1, hh, :], ident)
                        ins.then_inc(at2_ps[a], 1)
                pe.wait_ge(ao_sb[a], n)
                src = att_o[a].rearrange("p (q c) -> p c q", c=C)
                for c in range(C):
                    ins = pe.transpose(ps[:, 1, c * P:(c + 1) * P], src[:, c, :], ident)
                ins.then_inc(aoT_ps[a], 1)
                pe.wait_ge(aoT_sb[a], 1)
                for c in range(C):
                    ins = pe.matmul(ps[:, 2, :], att_oT[a][:, c, :], e_wo[:, c, :], start=(c == 0), stop=(c == C - 1))
                ins.then_inc(ap_ps[a], 1)

            attention(0)

            x_transposes(2)
            pe.wait_ge(xT_ready, 3)
            pe.wait_ge(ld_gw, 16)
            for c in range(C):
                ins = pe.matmul(ps[:, 0, 0:E0], xnT[:, c, :], gatew[:, c, :], start=(c == 0), stop=(c == C - 1))
            ins.then_inc(r_ps, 1)

            def gate_up(p, j, turn, first=False):
                pe.wait_ge(ld_ring[j], 16 * (turn + 1))
                if not first:
                    pe.wait_ge(h_done, p - 1)
                for bank, w, done in ((2 + j % 2, slot_gate[j], g_ps), (4 + j % 2, slot_up[j], u_ps)):
                    for c in range(C):
                        ins = pe.matmul(ps[:, bank, 0:384].rearrange("p (e n) -> p e n", e=2), xnT[:, c, :], w[:, :, c, :],
                                        start=(c == 0), stop=(c == C - 1))
                    ins.then_inc(done, 1)

            def hidden_transposes(p, k, first=False):
                pe.wait_ge(h_done, p + 1)
                if not first:
                    pe.wait_ge(hT_sb, p)
                src = moe_h[k].rearrange("p (q c) -> p c q", c=3)
                for c in range(3):
                    ins = pe.transpose(ps[:, 6, c * P:(c + 1) * P], src[:, c, :], ident)
                ins.then_inc(hT_ps, 1)

            def down(p, j, first=False, last=False):
                pe.wait_ge(hT_sb, p + 1)
                for c in range(3):
                    ins = pe.matmul(ps[:, 7, :], moe_hT[j % 2][:, c, :], slot_down[j][:, c, :],
                                    start=(first and c == 0), stop=(last and c == 2))
                ins.then_inc(dn_done, 1)

            for p in range(PAIRS):
                gate_up(p, p % SLOTS, p // SLOTS, p < 2)
                if p == 0:
                    pe.wait_ge(sel_done, 1)
                    pe.matmul(ps[:, 1, 0:E0], upper, r_sel, start=True, stop=True).then_inc(pos_ps, 1)
                if p >= 2:
                    down(p - 2, (p - 2) % SLOTS, p == 2)
                if p >= 1:
                    hidden_transposes(p - 1, (p - 1) % 2, p == 1)
            down(PAIRS - 2, (PAIRS - 2) % SLOTS)
            hidden_transposes(PAIRS - 1, 1)
            down(PAIRS - 1, (PAIRS - 1) % SLOTS, last=True)

            attention(1)

            x_transposes(4)
            pe.wait_ge(xT_ready, 5)
            pe.wait_ge(ld_b1, 16)
            for t in range(4):
                for c in range(C):
                    ins = pe.matmul(ps[:, t, :], xnT[:, c, :], w_ret[:, c, t, :], start=(c == 0), stop=(c == C - 1))
                ins.then_inc(t_ps, 1)
            for t in range(2):
                pe.wait_ge(rot_done, t + 1)
                for c in range(C):
                    ins = pe.transpose(ps[:, 4 + t, c * P:(c + 1) * P], rot[:, t, c * P:(c + 1) * P], ident)
                ins.then_inc(ret_T_ps, 1)
            pe.wait_ge(ret_kT_sb, 1)
            for c in range(C):
                pe.wait_ge(qbd_done, c + 1)
                pe.matmul(ps[:, (6, 7, 0, 1)[c], :], ret_kT[:, c, :], ret_qbd[:, c].rearrange("p h t -> p (h t)"),
                          start=True, stop=True).then_inc(rs_ps, 1)
            pe.wait_ge(ret_v_sb, 1)
            for c in range(C):
                pe.wait_ge(ret_pT_sb, c + 1)
                for hh in range(4):
                    v0 = (4 * c + hh) * 32
                    ins = pe.matmul(ps[:, 4 + c, hh * P:hh * P + 96], ret_pT[:, c, hh, :], ret_v[:, v0:v0 + 96],
                                    start=True, stop=True)
                ins.then_inc(y_ps, 1)
            pe.wait_ge(ret_o_done, 1)
            src = ret_y.rearrange("p h d -> p (h d)").rearrange("p (q c) -> p c q", c=C)
            for c in range(C):
                ins = pe.transpose(ps[:, 0, c * P:(c + 1) * P], src[:, c, :], ident)
            ins.then_inc(ret_oT_ps, 1)
            pe.wait_ge(ret_oT_sb, 1)
            for c in range(C):
                ins = pe.matmul(ps[:, 1, :], ret_oT[:, c, :], w_proj[:, c, :], start=(c == 0), stop=(c == C - 1))
            ins.then_inc(proj_ps, 1)

            x_transposes(5)
            pe.wait_ge(xT_ready, 6)
            pe.wait_ge(ld_router, 16)
            for c in range(C):
                ins = pe.matmul(ps[:, 0, 0:P], xnT[:, c, :], router[:, c, :], start=(c == 0), stop=(c == C - 1))
            ins.then_inc(fr_ps, 1)

            def f1_chunk(n):
                if n == 0:
                    pe.wait_ge(ld_f1s, 16)
                    gate, up = f1_sgate, f1_sup
                else:
                    pe.wait_ge(ld_f1[n - 1], 16)
                    pe.wait_ge(ld_f1[3 + n], 16)
                    gate, up = f1_gate[:, n - 1], f1_up[:, n - 1]
                if n >= 2:
                    pe.wait_ge(fh, n - 1)
                for bank, w, done in ((1 + n % 2, gate, fg_ps), (3 + n % 2, up, fu_ps)):
                    for c in range(C):
                        ins = pe.matmul(ps[:, bank, :], xnT[:, c, :], w[:, c, :], start=(c == 0), stop=(c == C - 1))
                    ins.then_inc(done, 1)

            f1_chunk(0)
            pe.wait_ge(fcoef, 1)
            pe.transpose(ps[:, 0, 0:P], f1_coef, ident).then_inc(fcT_ps, 1)
            f1_chunk(1)
            pe.wait_ge(fcT_sb, 1)
            pe.wait_ge(mix_done, 1)
            pe.matmul(ps[:, 0, 0:8], f1_coefT, mix_w, start=True, stop=True).then_inc(fck_ps, 1)
            pe.wait_ge(fh, 1)
            src = f1_hs.rearrange("p (q c) -> p c q", c=C)
            for c in range(C):
                ins = pe.transpose(ps[:, 5, c * P:(c + 1) * P], src[:, c, :], ident)
            ins.then_inc(fhT_ps, 1)
            f1_chunk(2)
            pe.wait_ge(fhT_sb, 1)
            pe.wait_ge(ld_f1d, 16)
            for c in range(C):
                pe.matmul(ps[:, 7, :], f1_hsT[:, c, :], f1_swd[:, c, :], start=(c == 0), stop=False)
            f1_chunk(3)
            f1_chunk(4)
            pe.wait_ge(fm_done, 1)
            src = f1_m.rearrange("p (q c) -> p c q", c=2)
            for c in range(2):
                ins = pe.transpose(ps[:, 6, c * P:(c + 1) * P], src[:, c, :], ident)
            ins.then_inc(fmT_ps, 1)
            pe.wait_ge(fmT_sb, 1)
            for c in range(2):
                ins = pe.matmul(ps[:, 7, :], f1_mT[:, c, :], f1_wd[:, c, :], start=False, stop=(c == 1))
            ins.then_inc(fo_ps, 1)


def constants():
    f = np.float32
    t = np.arange(P)
    same = t[:, None] // S == t[None, :] // S
    c = np.zeros((P, K_N), f)
    c[:, K_ID:K_ID + P] = np.eye(P)
    c[:, K_MASK:K_MASK + P] = np.where(same & (t[:, None] >= t[None, :]), 0.0, -1e30)
    c[:, K_U:K_U + P] = t[:, None] < t[None, :]
    c[:, K_IOTA:K_IOTA + P] = t[None, :]
    c[:, K_M16:K_M16 + 8] = t[:, None] // 16 == np.arange(8)[None, :]
    c[:, K_M32:K_M32 + 4] = t[:, None] // 32 == np.arange(4)[None, :]
    inv = (f(1.0) / np.power(f(10000.0), np.arange(0, P, 2, dtype=f) / f(P))).astype(f)
    fr = (np.arange(L, dtype=f)[:, None] * inv[None, :]).astype(f)
    cos = np.repeat(np.cos(fr), 2, axis=-1)
    sin = np.repeat(np.sin(fr), 2, axis=-1)
    sin[:, 0:P // 2] *= -1
    rope = np.concatenate([cos.reshape(P, J * P), sin.reshape(P, J * P)], axis=1).astype(f)
    ar = np.arange(0, D, 2, dtype=f)
    dim_scale = ((ar + f(0.4 * D)) / f(1.4 * D)).astype(f)
    pos = np.arange(S, dtype=f)
    scale = (dim_scale[None, :] ** (pos[:, None] / f(512.0))).astype(f)
    inv = (f(1.0) / np.power(f(10000.0), ar / f(D))).astype(f)
    sc = (pos[:, None] * inv[None, :]).astype(f)
    xs = np.repeat(np.sin(sc) * scale, 2, axis=-1)
    xc = np.repeat(np.cos(sc) * scale, 2, axis=-1)
    xs[:, 0::2] *= -1
    xpos = np.tile(np.concatenate([xc, xs], axis=1), (B, 1)).astype(f)
    gamma = (f(1.0) - f(2.0) ** (f(-5.0) - np.arange(16, dtype=f))).astype(f)
    diff = t[None, :] - t[:, None]
    ok = same & (diff >= 0)
    dec = np.where(ok[:, None, :], gamma[None, :, None] ** np.where(diff >= 0, diff, 0).astype(f)[:, None, :], f(0.0))
    decay = (dec.astype(f) * f(32.0) ** f(-0.5)).astype(f).reshape(P, 16 * P)
    return c, rope, xpos, decay


def rows(w, c):
    return w.reshape(P, -1)


def kernel(**inputs):
    import concourse.bacc as _bacc
    from concourse.bass_utils import run_bass_kernel_spmd as _run

    v = {k: np.asarray(a) for k, a in inputs.items()}
    ac = np.ascontiguousarray
    cst, rope, xpos, decay = constants()
    wq = v["L0_xattn_Wq"].T.reshape(P, C, GROUPS, 512)
    wkcq = v["L0_xattn_w_kc_q"].transpose(2, 0, 1).reshape(P, KQ, H0, P)
    wqr = v["L0_xattn_W_qr"].transpose(1, 0, 2).reshape(P, KQ, H0, R0)
    wa = np.stack([np.concatenate([wq[:, :, g].reshape(P, -1),
                                   wkcq[:, :, 4 * g:4 * g + 4].transpose(0, 2, 1, 3).reshape(P, -1),
                                   wqr[:, :, 4 * g:4 * g + 4].transpose(0, 2, 1, 3).reshape(P, -1)], axis=1)
                   for g in range(GROUPS)])
    wkr = v["L0_xattn_W_kr"].transpose(2, 0, 1).reshape(R0, H0 * P)
    wb = np.concatenate([v["L0_xattn_Wo"].T.reshape(H0, P, D).transpose(1, 0, 2).reshape(P, -1),
                         v["L0_xattn_w_kc_kv"].transpose(2, 0, 1).reshape(P, -1)], axis=1)
    q0 = v["L0_attn_wq"].T.reshape(D, 8, 4, 16).transpose(0, 2, 1, 3).reshape(D, D)
    e0 = np.concatenate([q0.reshape(P, -1), v["L0_attn_wk"].T.reshape(P, -1), v["L0_attn_wv"].T.reshape(P, -1),
                         v["L0_attn_wo"].T.reshape(P, -1)], axis=1)
    pair = lambda w: w.reshape(PAIRS, 2, P, C, I0).transpose(0, 2, 1, 3, 4).reshape(PAIRS, P, -1)
    ring = np.concatenate([pair(v["L0_ffn_w_gate"]), pair(v["L0_ffn_w_up"]),
                           v["L0_ffn_w_down"].reshape(PAIRS, P, 3 * D)], axis=2)
    kv1 = v["L1_xattn_Wkv_expand"].T
    e1 = np.concatenate([v["L1_xattn_Wq"].T.reshape(P, -1), kv1, v["L1_xattn_Wout"].T.reshape(P, -1)], axis=1)
    b1 = np.concatenate([np.concatenate([v["L1_attn_w_qkv"], v["L1_attn_w_g"]], axis=1).reshape(P, -1),
                         v["L1_attn_w_proj"].reshape(P, -1)], axis=1)
    gn = np.stack([v["L1_attn_gn_weight"], v["L1_attn_gn_bias"]])
    chunk = lambda w: w.reshape(P, C, 4, 512).transpose(2, 0, 1, 3)
    f1gu = np.concatenate([chunk(v["L1_ffn_w_gate"]), chunk(v["L1_ffn_w_up"])])
    f1s = np.concatenate([v["L1_ffn_shared_w_gate"].reshape(P, -1), v["L1_ffn_shared_w_up"].reshape(P, -1)], axis=1)
    f1d = np.concatenate([v["L1_ffn_w_down"].reshape(P, -1), v["L1_ffn_shared_w_down"].reshape(P, -1)], axis=1)
    ctx = v["ctx_512"]
    arrays = {
        "x": v["x"].reshape(P, D), "consts": cst, "rope": rope,
        "ctx": ctx.reshape(B, P, J * P).transpose(1, 0, 2).reshape(P, -1), "ctx64": ctx[:, 0:S].reshape(P, P),
        "wa": wa, "wkr": wkr, "wb": wb, "e0": e0, "gatew": v["L0_ffn_gate_w"].reshape(P, -1), "ring": ring, "e1": e1,
        "b1": b1, "xpos": xpos, "gn": gn, "decay": decay, "f1gu": f1gu, "f1s": f1s, "f1d": f1d,
        "router": v["L1_ffn_w_router"].reshape(P, -1), "escale": v["L1_ffn_expert_scale"].reshape(1, P),
        "amp": v["L1_ffn_amplitudes"],
    }
    nc = _bacc.Bacc("TRN2", target_bir_lowering=False, num_devices=1)
    ins, args = {}, []
    for name, a in arrays.items():
        a = ac(a)
        ins[f"in_{name}"] = a
        args.append(nc.dram_tensor(f"in_{name}", a.shape, mybir.dt.from_np(a.dtype), kind="ExternalInput").ap())
    out = nc.dram_tensor("out_x", (P, D), F32, kind="ExternalOutput").ap()
    build(nc, *args, out)
    r = _run(nc, [ins], core_ids=[0])
    return r.results[0]["out_x"].reshape(B, S, D)
```

```python
from contextlib import ExitStack

import numpy as np
import concourse.bass as bass
from concourse import mybir

F32 = mybir.dt.float32
BF16 = mybir.dt.bfloat16
U32 = mybir.dt.uint32
ALU = mybir.AluOpType
ACT = mybir.ActivationFunctionType
AX = mybir.AxisListType

P = 128
B, S, D = 2, 64, 512
C = D // P
L = 1024
H0, R0, DQ = 16, 64, 384
KQ = DQ // P
GROUPS = H0 // 4
UNITS = H0 * S * B // P
J = L // P
E0, I0, CAP = 32, 192, 64
PAIRS = E0 // 2
SLOTS = 4
DENSE = 2
PLACED = (E0 - 2 * DENSE) * CAP
EPS = 1e-5
LN_WARM = 26

PAIR_GU = 2 * C * I0
PAIR_N = 2 * PAIR_GU + 3 * D

A_G = C * 512 + 4 * KQ * P + 4 * KQ * R0
A_R = 4 * KQ * (P + R0)
A_N = GROUPS * A_G
B_N = H0 * D + H0 * P
D_N = 19968

K_ID, K_MASK, K_U, K_IOTA, K_M16, K_M32, K_N = 0, 128, 256, 384, 512, 520, 524


def build(nc, x_in, consts_d, rope_d, ctx_d, ctx64_d, wr_d, wq_d, wkr_d, wb_d, e0_d, gatew_d, ring_d, e1_d, b1_d,
          xpos_d, gn_d, decay_d, f1gu_d, f1s_d, f1d_d, router_d, escale_d, amp_d, out_d):
    with ExitStack() as stack:
        def sb(name, shape, dt=F32):
            return stack.enter_context(nc.sbuf_tensor(name, shape, dt))

        def sem(name):
            return stack.enter_context(nc.semaphore(name))

        ra = sb("ra", [P, A_N])
        rb = sb("rb", [P, B_N])
        rd = sb("rd", [P, D_N])
        x = sb("x", [P, D])
        xn = sb("xn", [P, D])
        xnT = sb("xnT", [P, C, P])
        cst = sb("cst", [P, K_N])
        identb = sb("identb", [P, P], BF16)
        maskb = sb("maskb", [P, 4, P], BF16)
        ones = sb("ones", [P, P])
        xpos = sb("xpos", [P, 2, D])
        gnwb = sb("gnwb", [P, 2, D])
        ctx64 = sb("ctx64", [P, P])
        ctx64T = sb("ctx64T", [P, P])
        gatew = sb("gatew", [P, C, E0])
        escale = sb("escale", [P, P])
        amp = sb("amp", [P, 8, 2])
        sv = sb("sv", [P, 332])
        top8i = sb("top8i", [P, 8], U32)
        ps = stack.enter_context(nc.psum_tensor("ps", [P, 8, 512], F32))

        ident = cst[:, K_ID:K_ID + P]
        maskf = cst[:, K_MASK:K_MASK + P]
        upper = cst[:, K_U:K_U + P]
        iota = cst[:, K_IOTA:K_IOTA + P]
        m16 = cst[:, K_M16:K_M16 + 8]
        m32 = cst[:, K_M32:K_M32 + 4]

        def wq_x(g):
            o = g * A_G + A_R
            return ra[:, o:o + 2048].rearrange("p (c n) -> p c n", c=C)

        def wkcq(g):
            o = g * A_G
            return ra[:, o:o + 1536].rearrange("p (h c k) -> p h c k", h=4, c=KQ)

        def wqr(g):
            o = g * A_G + 4 * KQ * P
            return ra[:, o:o + 768].rearrange("p (h c r) -> p h c r", h=4, c=KQ)

        wo_x = rb[:, 0:8192].rearrange("p (h n) -> p h n", h=H0)
        wkv_x = rb[:, 8192:10240].rearrange("p (h k) -> p h k", h=H0)
        ctxr = rd[:, 0:2048].rearrange("p (b j d) -> p b j d", b=B, j=J)
        rope_cos = rd[:, 2048:2560].rearrange("p (j i) -> p j i", j=J)
        rope_sin = rd[:, 2560:3072].rearrange("p (j i) -> p j i", j=J)
        rope_tmp = rd[:, 4096:5120].rearrange("p (j d) -> p j d", j=J)
        qT_x = rd[:, 5120:7168].rearrange("p (h t) -> p h t", h=H0)
        qrk = rd[:, 7168:9216].rearrange("p (h k) -> p h k", h=H0)
        qkw = rd[:, 9216:11264].rearrange("p (h d) -> p h d", h=H0)
        wkrT = rd[:, 11264:13312].rearrange("p (h d) -> p h d", h=H0)
        kvr = rd[:, 13824:15872].rearrange("p (b j d) -> p b j d", b=B, j=J)
        kvT = rd[:, 15872:17920].rearrange("p (b l) -> p b l", b=B)
        qk_x = rd[:, 17920:19968].rearrange("p (b h s) -> p b h s", b=B, h=H0)
        prob_x = [ra[:, 1024 * i:1024 * i + 1024].rearrange("p (j l) -> p j l", j=J) for i in range(2)]
        probT_x = [ra[:, 2048 + 1024 * i:3072 + 1024 * i].rearrange("p (j r) -> p j r", j=J) for i in range(2)]
        ctxT = ra[:, 4096:6144].rearrange("p (h b s) -> p h b s", h=H0, b=B)
        latT = ra[:, 11264:13312].rearrange("p (h t) -> p h t", h=H0)
        we = ra[:, 6144:11264]
        e_wq = we[:, 0:2048].rearrange("p (c n) -> p c n", c=C)
        e_wk0 = we[:, 2048:2560].rearrange("p (c n) -> p c n", c=C)
        e_wv0 = we[:, 2560:3072].rearrange("p (c n) -> p c n", c=C)
        e_wk1 = we[:, 2048:2560]
        e_wv1 = we[:, 2560:3072]
        e_wo = we[:, 3072:5120].rearrange("p (c n) -> p c n", c=C)
        att_banks = [8, 4]
        att_hd = [16, 32]
        att_prob = [ra[:, 0:4096].rearrange("p (i h t) -> p i h t", i=8, h=4),
                    ra[:, 0:2048].rearrange("p (i h t) -> p i h t", i=4, h=4)]
        att_probT = [rb[:, 0:4096].rearrange("p (i h t) -> p i h t", i=8, h=4),
                     ra[:, 2048:4096].rearrange("p (i h t) -> p i h t", i=4, h=4)]
        att_kbd = [ra[:, 4096:5120].rearrange("p (h t) -> p h t", h=8),
                   ra[:, 4096:6144].rearrange("p (h t) -> p h t", h=16)]
        att_qT = [ra[:, 5120:5632].rearrange("p (i t) -> p i t", i=4),
                  ra[:, 11856:12368].rearrange("p (i t) -> p i t", i=4)]
        att_v = [ra[:, 5632:5848], ra[:, 11264:11856]]
        att_o = [rb[:, 4096:4608], ra[:, 12368:12880]]
        att_oT = [rb[:, 4608:5120].rearrange("p (c t) -> p c t", c=C),
                  ra[:, 11856:12368].rearrange("p (c t) -> p c t", c=C)]
        slot = [rd[:, PAIR_N * j:PAIR_N * (j + 1)] for j in range(SLOTS)]
        slot_gate = [s[:, 0:PAIR_GU].rearrange("p (e c n) -> p e c n", e=2, c=C) for s in slot]
        slot_up = [s[:, PAIR_GU:2 * PAIR_GU].rearrange("p (e c n) -> p e c n", e=2, c=C) for s in slot]
        slot_gu = [s[:, 0:2 * PAIR_GU].rearrange("p (g e c n) -> p g e c n", g=2, e=2, c=C) for s in slot]
        slot_down = [s[:, 2 * PAIR_GU:PAIR_N].rearrange("p (c n) -> p c n", c=3) for s in slot]
        moe_th = [ra[:, 384 * i:384 * i + 384] for i in range(2)]
        moe_a = ra[:, 768:1152]
        moe_h = [ra[:, 1152 + 384 * i:1536 + 384 * i] for i in range(2)]
        moe_hq = [ra[:, 1920 + 256 * i:2176 + 256 * i] for i in range(2)]
        moe_hT_even = [ra[:, 2432 + 512 * i:2944 + 512 * i].rearrange("p (c t) -> p c t", c=4) for i in range(2)]
        moe_hT_odd = [ra[:, 3456 + 256 * i:3712 + 256 * i].rearrange("p (c t) -> p c t", c=2) for i in range(2)]
        placed = ra[:, 3968:3968 + PLACED].rearrange("p (e s) -> p e s", s=CAP)
        moe_xq = [ra[:, 11264 + 1024 * i:12288 + 1024 * i].rearrange("p (c n) -> p c n", c=C) for i in range(2)]
        placed_w = [rd[:, 18432 + 256 * i:18688 + 256 * i].rearrange("p (e s) -> p e s", s=CAP) for i in range(2)]
        moe_y = xnT[:, :, :].rearrange("p c t -> p (c t)")
        w_ret = rb[:, 0:8192].rearrange("p (c t n) -> p c t n", c=C, t=4)
        w_proj = rb[:, 8192:10240].rearrange("p (c n) -> p c n", c=C)
        rot = ra[:, 0:1024].rearrange("p (t n) -> p t n", t=2)
        rot_tmp = ra[:, 1024:2048].rearrange("p (t n) -> p t n", t=2)
        ret_v = ra[:, 2048:2624]
        ret_kT = ra[:, 2624:3136].rearrange("p (c t) -> p c t", c=C)
        ret_th = ra[:, 3136:3648]
        ret_ag = ra[:, 3648:4160]
        ret_qbd = ra[:, 4160:6208].rearrange("p (c h t) -> p c h t", c=C, h=4)
        ret_pT = ra[:, 6208:8256].rearrange("p (c h t) -> p c h t", c=C, h=4)
        ret_y = ra[:, 8256:8768].rearrange("p (h d) -> p h d", h=16)
        ret_sq = ra[:, 8768:9280].rearrange("p (h d) -> p h d", h=16)
        ret_aw = ra[:, 9792:10304]
        ret_ab = ra[:, 10304:10816]
        ret_oT = ra[:, 9280:9792].rearrange("p (c t) -> p c t", c=C)
        decay = ra[:, 11264:13312].rearrange("p (c n) -> p c n", c=C)
        f1_gate = rd[:, 0:8192].rearrange("p (n c i) -> p n c i", n=4, c=C)
        f1_up = rd[:, 8192:16384].rearrange("p (n c i) -> p n c i", n=4, c=C)
        f1_wd = rd[:, 16384:17408].rearrange("p (c n) -> p c n", c=2)
        f1_swd = rd[:, 17408:19456].rearrange("p (c n) -> p c n", c=C)
        router = rd[:, 19456:19968].rearrange("p (c n) -> p c n", c=C)
        f1_sgate = ra[:, 13312:15360].rearrange("p (c n) -> p c n", c=C)
        f1_sup = ra[:, 15360:17408].rearrange("p (c n) -> p c n", c=C)
        f1_th = [ra[:, 512 * i:512 * i + 512] for i in range(2)]
        f1_a = ra[:, 1024:1536]
        f1_hs = ra[:, 1536:2048]
        f1_hsT = ra[:, 2048:2560].rearrange("p (c t) -> p c t", c=C)
        f1_b = ra[:, 2560:4608].rearrange("p (k i) -> p k i", k=8)
        f1_m = ra[:, 4608:4864]
        f1_mT = ra[:, 4864:5120].rearrange("p (c t) -> p c t", c=2)
        f1_e = ra[:, 5120:5248]
        f1_sel = ra[:, 5248:5376]
        f1_coef = ra[:, 5376:5504]
        f1_coefT = ra[:, 5504:5632]

        stats = sv[:, 0:6]
        mv = sv[:, 6:8]
        rstd = sv[:, 8:9]
        neghalf = sv[:, 9:10]
        var_eps = sv[:, 10:11]
        mx_x = sv[:, 12:28]
        rs_x = sv[:, 28:44]
        rr_x = sv[:, 44:60]
        asum = sv[:, 60:64]
        wscale = sv[:, 64:68]
        sc_qk = sv[:, 68:69]
        sc_vo = sv[:, 69:70]
        att_mx = [sv[:, 70:74], sv[:, 314:318]]
        att_rec = [sv[:, 74:78], sv[:, 318:322]]
        r_mx = sv[:, 78:79]
        top8 = sv[:, 79:87]
        r_sum = sv[:, 87:88]
        r_z = sv[:, 88:89]
        r_rec = sv[:, 89:90]
        top8f = sv[:, 90:98]
        r_e = sv[:, 98:130]
        r_rep = sv[:, 130:162]
        r_sel = sv[:, 162:194]
        r_em = sv[:, 194:226]
        coef = sv[:, 226:258]
        g_mean = sv[:, 258:274]
        g_var = sv[:, 274:290]
        ck = sv[:, 306:314]
        mix = sb("mix", [P, 24])
        mix_p, mix_w = mix[:, 0:8], mix[:, 8:16]
        mix_s, mix_r = mix[:, 16:17], mix[:, 17:18]
        r_place = sb("r_place", [P, E0])[:, :]
        g_rstd = sb("g_rstd", [P, 16])

        ld_x, ld_const, ld_ctx, ld_kr, ld_b0, ld_c64 = map(sem, ("ld_x", "ld_const", "ld_ctx", "ld_kr", "ld_b0", "ld_c64"))
        ld_r = [sem(f"ld_r{g}") for g in range(GROUPS)]
        ld_q = [sem(f"ld_q{g}") for g in range(GROUPS)]
        ld_e0, ld_gw, ld_e1, ld_b1, ld_late, ld_decay = map(sem, ("ld_e0", "ld_gw", "ld_e1", "ld_b1", "ld_late", "ld_decay"))
        late_loads = 4
        ld_ring = [sem(f"ld_ring{j}") for j in range(SLOTS)]
        ld_f1 = [sem(f"ld_f1_{n}") for n in range(4)]
        ld_f1s, ld_f1d, ld_router = map(sem, ("ld_f1s", "ld_f1d", "ld_router"))
        st_out = sem("st_out")
        dve_step, pool_step = sem("dve_step"), sem("pool_step")
        consts_ready = sem("consts_ready")
        var_ready, rstd_ready, xn_ready, xT_ps, xT_ready = map(sem, ("var_ready", "rstd_ready", "xn_ready", "xT_ps", "xT_ready"))
        rope_ready, rope_swap, c64T_ps, c64T_ready = map(sem, ("rope_ready", "rope_swap", "c64T_ps", "c64T_ready"))
        at_ps, at_sb, q_ps, q_sb, bw_ps, bw_sb, qk_ps, qk_sb, kvT_ps, kvT_sb = map(
            sem, ("at_ps", "at_sb", "q_ps", "q_sb", "bw_ps", "bw_sb", "qk_ps", "qk_sb", "kvT_ps", "kvT_sb"))
        s_ps, mx_done, exp_done, pt_ps, pt_sb0, pt_sb1, ctx_ps, ctx_sb, cT_ps, cT_sb, lat_ps, lat_sb0, lat_sb1, o_ps = map(
            sem, ("s_ps", "mx_done", "exp_done", "pt_ps", "pt_sb0", "pt_sb1", "ctx_ps", "ctx_sb", "cT_ps", "cT_sb", "lat_ps",
                  "lat_sb0", "lat_sb1", "o_ps"))
        asum_done, sign_done, wsum_ps, wscale_done = map(sem, ("asum_done", "sign_done", "wsum_ps", "wscale_done"))
        aq_ps, aq_sb, akv_ps, ak_sb, av_sb, as_ps, asub, aexp, at2_ps, at2_sb, ao_ps, ao_sb, aoT_ps, aoT_sb, ap_ps = (
            [sem(f"{n}{i}") for i in range(2)] for n in
            ("aq_ps", "aq_sb", "akv_ps", "ak_sb", "av_sb", "as_ps", "asub", "aexp", "apt_ps", "apt_sb", "ao_ps", "ao_sb",
             "aoT_ps", "aoT_sb", "aproj_ps"))
        res_done = sem("res_done")
        r_ps, rmx_done, rexp_done, sel_done, pos_ps, places_done = map(
            sem, ("r_ps", "rmx_done", "rexp_done", "sel_done", "pos_ps", "places_done"))
        g_ps, u_ps, th_done, h_done, hT_ps, hT_sb, dn_done = map(
            sem, ("g_ps", "u_ps", "th_done", "h_done", "hT_ps", "hT_sb", "dn_done"))
        placed_w_done, xq_ps, xq_sb, y_sb, moe_done = map(sem, ("placed_w_done", "xq_ps", "xq_sb", "y_sb", "moe_done"))
        t_ps, rot_done, ret_v_sb, ret_th_done, ret_T_ps, ret_kT_sb, qbd_done, rs_ps, ret_pT_sb, y_ps, gvar_done, gsqrt_done = map(
            sem, ("t_ps", "rot_done", "ret_v_sb", "ret_th_done", "ret_T_ps", "ret_kT_sb", "qbd_done", "rs_ps", "ret_pT_sb", "y_ps",
                  "gvar_done", "gsqrt_done"))
        ret_o_done, ret_oT_ps, ret_oT_sb, proj_ps, ag_done = map(
            sem, ("ret_o_done", "ret_oT_ps", "ret_oT_sb", "proj_ps", "ag_done"))
        fr_ps, frmx, frexp, fcoef, fcT_ps, fcT_sb, fck_ps, mix_done = map(
            sem, ("fr_ps", "frmx", "frexp", "fcoef", "fcT_ps", "fcT_sb", "fck_ps", "mix_done"))
        fg_ps, fu_ps, fth, fh, fhT_ps, fhT_sb, fm_done, fmT_ps, fmT_sb, fo_ps = map(
            sem, ("fg_ps", "fu_ps", "fth", "fh", "fhT_ps", "fhT_sb", "fm_done", "fmT_ps", "fmT_sb", "fo_ps"))

        block = stack.enter_context(nc.Block())

        @block.sync
        def _(sp):
            def rank_weights(g):
                sp.dma_start(ra[:, g * A_G:g * A_G + A_R], wr_d[g]).then_inc(ld_r[g], 16)

            def query_weights(g):
                sp.dma_start(ra[:, g * A_G + A_R:(g + 1) * A_G], wq_d[g]).then_inc(ld_q[g], 16)

            sp.dma_start(x[:, :], x_in).then_inc(ld_x, 16)
            rank_weights(0)
            sp.dma_start(cst[:, :], consts_d).then_inc(ld_const, 16)
            query_weights(0)
            sp.dma_start(rd[0:R0, 11264:13312], wkr_d).then_inc(ld_kr, 16)
            rank_weights(1)
            sp.dma_start(rd[:, 0:2048], ctx_d).then_inc(ld_ctx, 16)
            sp.dma_start(rd[:, 2048:3072], rope_d).then_inc(ld_ctx, 16)
            for g in range(1, GROUPS):
                if g > 1:
                    rank_weights(g)
                query_weights(g)
            sp.dma_start(ctx64[:, :], ctx64_d).then_inc(ld_c64, 16)
            sp.dma_start(rb[:, :], wb_d).then_inc(ld_b0, 16)
            sp.dma_start(gatew[:, :, :], gatew_d.rearrange("p (c n) -> p c n", c=C)).then_inc(ld_gw, 16)
            sp.wait_ge(qk_ps, GROUPS)
            sp.dma_start(we, e0_d).then_inc(ld_e0, 16)
            for j in range(3):
                sp.dma_start(slot[j], ring_d[j]).then_inc(ld_ring[j], 16)
            sp.dma_start(ra[:, 13312:17408], f1s_d).then_inc(ld_f1s, 16)
            sp.dma_start(xpos[:, :, :], xpos_d.rearrange("p (t n) -> p t n", t=2)).then_inc(ld_late, 16)
            sp.dma_start(gnwb[:, :, :], gn_d.rearrange("(a t) n -> a t n", a=1).broadcast_to([P, 2, D])).then_inc(ld_late, 16)
            sp.dma_start(escale[:, :], escale_d.broadcast_to([P, P])).then_inc(ld_late, 16)
            sp.dma_start(amp[:, :, :], amp_d).then_inc(ld_late, 16)
            sp.wait_ge(ctx_ps, UNITS)
            sp.dma_start(slot[3], ring_d[3]).then_inc(ld_ring[3], 16)
            sp.wait_ge(res_done, 2)
            sp.dma_start(we, e1_d).then_inc(ld_e1, 16)

            def refill(p, j):
                sp.wait_ge(dn_done, p - (SLOTS - 1))
                sp.dma_start(slot[j], ring_d[p]).then_inc(ld_ring[j], 16)

            for p in range(SLOTS, PAIRS):
                refill(p, p % SLOTS)
            sp.dma_start(rb[:, :], b1_d).then_inc(ld_b1, 16)
            sp.wait_ge(dn_done, PAIRS)
            sp.dma_start(rd[:, 19456:19968], router_d).then_inc(ld_router, 16)
            for n in range(4):
                sp.dma_start(f1_gate[:, n], f1gu_d[n]).then_inc(ld_f1[n], 16)
                sp.dma_start(f1_up[:, n], f1gu_d[4 + n]).then_inc(ld_f1[n], 16)
            sp.dma_start(rd[:, 16384:19456], f1d_d).then_inc(ld_f1d, 16)
            sp.wait_ge(res_done, 4)
            sp.dma_start(ra[:, 11264:13312], decay_d).then_inc(ld_decay, 16)
            sp.wait_ge(res_done, 6)
            sp.dma_start(out_d, x[:, :]).then_inc(st_out, 16)
            sp.wait_ge(st_out, 16)

        @block.gpsimd
        def _(pool):
            steps = [0]

            def link(ins):
                steps[0] += 1
                ins.then_inc(pool_step, 1)
                pool.wait_ge(pool_step, steps[0])

            pool.memset(ones[:, :], 1.0).then_inc(consts_ready, 1)
            link(pool.memset(neghalf, -0.5))

            def rstd_of(i):
                pool.wait_ge(var_ready, i + 1)
                link(pool.tensor_scalar(var_eps, mv[:, 1:2], EPS, None, ALU.add))
                pool.tensor_tensor(rstd, var_eps, neghalf, ALU.pow).then_inc(rstd_ready, 1)

            rstd_of(0)
            pool.wait_ge(ld_ctx, 2 * 16)
            for b in range(B):
                if b:
                    pool.wait_ge(rope_ready, b)
                for half in range(2):
                    dst = rope_tmp[:, :, 64 * half:64 * half + 64].rearrange("p j (i two) -> p j i two", two=2)
                    src = ctxr[:, b, :, 64 - 64 * half:128 - 64 * half].rearrange("p j (i two) -> p j i two", two=2)
                    sin = rope_sin[:, :, 32 * half:32 * half + 32].unsqueeze(3).broadcast_to([P, J, 32, 2])
                    ins = pool.tensor_tensor(dst, src, sin, ALU.mult)
                ins.then_inc(rope_swap, 1)
            rstd_of(1)
            rstd_of(2)
            for h in moe_hq:
                link(pool.memset(h, 0.0))
            pool.wait_ge(places_done, 2)
            for q in range(PAIRS // 2 - 1):
                if q >= 2:
                    pool.wait_ge(hT_ps, 2 * q - 1)
                pool.tensor_tensor(placed_w[q % 2], placed[:, 4 * q:4 * q + 4, :],
                                   coef[:, 2 * DENSE + 4 * q:2 * DENSE + 4 * q + 4].unsqueeze(2).broadcast_to([P, 4, CAP]),
                                   ALU.mult).then_inc(placed_w_done, 1)
            for i in range(3, 6):
                rstd_of(i)
            pool.wait_ge(fh, 2)
            link(pool.tensor_tensor(f1_m, f1_b[:, 0, :], f1_b[:, 1, :], ALU.add))
            for n in range(1, 4):
                pool.wait_ge(fh, n + 2)
                for k in (2 * n, 2 * n + 1):
                    if k < 7:
                        link(pool.tensor_tensor(f1_m, f1_m, f1_b[:, k, :], ALU.add))
            pool.tensor_tensor(f1_m, f1_m, f1_b[:, 7, :], ALU.add).then_inc(fm_done, 1)

        @block.scalar
        def _(act):
            def kvT_copy(g):
                act.wait_ge(kvT_ps, g + 1)
                dst = kvT[:, g // 2, (g % 2) * 512:(g % 2) * 512 + 512]
                act.activation(dst, ps[:, 7, :], ACT.Copy).then_inc(kvT_sb, 1)

            for g in range(GROUPS):
                act.wait_ge(q_ps, g + 1)
                act.activation(qT_x[:, 4 * g:4 * g + 4, :].rearrange("p h t -> p (h t)"), ps[:, g % 2, :],
                               ACT.Copy).then_inc(q_sb, 1)
                if g == 1:
                    kvT_copy(0)
                if g == 2:
                    kvT_copy(1)
                    kvT_copy(2)
            kvT_copy(3)

            def exp_unit(u):
                act.wait_ge(mx_done, u + 1)
                if u >= 2:
                    act.wait_ge(pt_ps, 2 * (u - 1))
                act.activation(prob_x[u % 2].rearrange("p j l -> p (j l)"),
                               ps[:, 2 * (u % 2):2 * (u % 2) + 2, :].rearrange("p a n -> p (a n)"), ACT.Exp,
                               bias=mx_x[:, u:u + 1], accum_out=rs_x[:, u:u + 1]).then_inc(exp_done, 1)

            def probT_copy(u):
                act.wait_ge(pt_ps, 2 * u + 1)
                if u >= 2:
                    act.wait_ge(ctx_ps, u - 1)
                act.activation(probT_x[u % 2][:, 0:4, :].rearrange("p j r -> p (j r)"), ps[:, 4, :],
                               ACT.Copy).then_inc(pt_sb0, 1)

            def ctxT_copy(u):
                act.wait_ge(cT_ps, u + 1)
                act.activation(ctxT[:, 2 * (u // 2):2 * (u // 2) + 2, u % 2, :],
                               ps[:, 7, 0:P].rearrange("p (h s) -> p h s", h=2), ACT.Copy).then_inc(cT_sb, 1)

            def latT_copy(g):
                act.wait_ge(lat_ps, g + 1)
                act.activation(latT[:, 4 * g:4 * g + 4, :].rearrange("p h t -> p (h t)"), ps[:, g, :],
                               ACT.Copy).then_inc(lat_sb0, 1)

            for i in range(UNITS + 3):
                if i < UNITS:
                    exp_unit(i)
                if 1 <= i <= UNITS:
                    probT_copy(i - 1)
                if i == UNITS + 2:
                    latT_copy(0)
                if i >= 3:
                    ctxT_copy(i - 3)
                if i == 12:
                    act.wait_ge(asum_done, 4)
                    act.activation(we, we, ACT.Sign).then_inc(sign_done, 1)
            latT_copy(2)

            def attention(a):
                n = att_banks[a]
                act.wait_ge(aq_ps[a], 1)
                act.activation(att_qT[a].rearrange("p i t -> p (i t)"), ps[:, 0, :], ACT.Copy).then_inc(aq_sb[a], 1)
                if a == 0:
                    act.wait_ge(wscale_done, 1)
                for i in range(n + 2):
                    if i < n:
                        act.wait_ge(asub[a], i + 1)
                        p = att_prob[a][:, i].rearrange("p h t -> p (h t)")
                        act.activation(p, p, ACT.Exp, scale=sc_qk if a == 0 else att_hd[a] ** -0.5).then_inc(aexp[a], 1)
                    if i >= 2:
                        act.wait_ge(at2_ps[a], i - 1)
                        act.activation(att_probT[a][:, i - 2].rearrange("p h t -> p (h t)"), ps[:, 5 + i % 2, :],
                                       ACT.Copy).then_inc(at2_sb[a], 1)

            attention(0)

            act.wait_ge(rmx_done, 1)
            act.activation(r_e, ps[:, 0, 0:E0], ACT.Exp, bias=r_mx).then_inc(rexp_done, 1)

            def moe_tanh(p, k):
                act.wait_ge(g_ps, p + 1)
                act.activation(moe_th[k], ps[:, 2 + k, 0:384], ACT.Tanh, scale=0.5).then_inc(th_done, 1)

            def moe_hT_copy(p, k):
                act.wait_ge(hT_ps, p + 1)
                act.activation(moe_hT_even[k][:, 0:3, :].rearrange("p c t -> p (c t)"), ps[:, 6, 0:384],
                               ACT.Copy).then_inc(hT_sb, 1)

            def xq_copy(q, half):
                act.wait_ge(xq_ps, 2 * q + half + 1)
                act.activation(moe_xq[q % 2][:, 2 * half:2 * half + 2, :].rearrange("p c n -> p (c n)"), ps[:, half, :],
                               ACT.Copy).then_inc(xq_sb, 1)

            def moe_tanh_queued(p):
                act.wait_ge(g_ps, p + 1)
                act.wait_ge(h_done, p - 1)
                act.activation(moe_th[p % 2][:, 0:I0], ps[:, 2 + p % 2, 0:I0], ACT.Tanh, scale=0.5).then_inc(th_done, 1)

            def moe_hT_copy_queued(p):
                act.wait_ge(hT_ps, p + 1)
                q = (p - DENSE) // 2
                dst, n = (moe_hT_even[q % 2], 512) if p % 2 == 0 else (moe_hT_odd[q % 2], 256)
                act.activation(dst.rearrange("p c t -> p (c t)"), ps[:, 6, 0:n], ACT.Copy).then_inc(hT_sb, 1)

            for p in range(PAIRS):
                if p < DENSE:
                    moe_tanh(p, p % 2)
                else:
                    moe_tanh_queued(p)
                if 1 <= p <= DENSE:
                    moe_hT_copy(p - 1, (p - 1) % 2)
                elif p > DENSE:
                    moe_hT_copy_queued(p - 1)
                if p == 1:
                    xq_copy(0, 0)
                    xq_copy(0, 1)
                elif 2 <= p < PAIRS - 2:
                    xq_copy(p // 2, p % 2)
            moe_hT_copy_queued(PAIRS - 1)

            attention(1)

            act.wait_ge(t_ps, 3)
            act.activation(ret_v[:, 0:512], ps[:, 2, :], ACT.Copy).then_inc(ret_v_sb, 1)
            act.wait_ge(t_ps, 4)
            act.activation(ret_th, ps[:, 3, :], ACT.Tanh, scale=0.5).then_inc(ret_th_done, 1)
            act.wait_ge(ret_T_ps, 2)
            act.activation(ret_kT.rearrange("p c t -> p (c t)"), ps[:, 5, :], ACT.Copy).then_inc(ret_kT_sb, 1)
            act.wait_ge(consts_ready, 2)
            act.activation(mix[:, 20:21], ones[:, 0:1], ACT.Sqrt)
            act.wait_ge(gvar_done, 1)
            act.activation(g_rstd[:, :], g_var, ACT.Sqrt).then_inc(gsqrt_done, 1)

            def f1_tanh(n):
                act.wait_ge(fg_ps, n + 1)
                if n >= 2:
                    act.wait_ge(fh, n - 1)
                act.activation(f1_th[n % 2], ps[:, 1 + n % 2, :], ACT.Tanh, scale=0.5).then_inc(fth, 1)

            act.wait_ge(frmx, 1)
            act.activation(f1_e, ps[:, 0, 0:P], ACT.Exp, bias=r_mx, accum_out=r_z).then_inc(frexp, 1)
            f1_tanh(0)
            f1_tanh(1)
            act.wait_ge(fhT_ps, 1)
            act.activation(f1_hsT.rearrange("p c t -> p (c t)"), ps[:, 5, :], ACT.Copy).then_inc(fhT_sb, 1)
            for n in range(2, 5):
                f1_tanh(n)
            act.wait_ge(fmT_ps, 1)
            act.activation(f1_mT.rearrange("p c t -> p (c t)"), ps[:, 6, 0:256], ACT.Copy).then_inc(fmT_sb, 1)

        @block.vector
        def _(dve):
            steps = [0]

            def link(ins):
                steps[0] += 1
                ins.then_inc(dve_step, 1)
                dve.wait_ge(dve_step, steps[0])

            def layernorm(i):
                link(dve.bn_stats(stats, x[:, :]))
                dve.bn_aggr(mv, stats).then_inc(var_ready, 1)
                dve.wait_ge(rstd_ready, i + 1)
                dve.tensor_scalar(xn[:, :], x[:, :], mv[:, 0:1], rstd, ALU.subtract, ALU.mult).then_inc(xn_ready, 1)

            def xT_copy(i):
                dve.wait_ge(xT_ps, i + 1)
                dve.tensor_copy(xnT[:, :, :].rearrange("p c t -> p (c t)"), ps[:, 7, :]).then_inc(xT_ready, 1)

            def add_residual(psum, scale=None):
                if scale is None:
                    dve.tensor_tensor(x[:, :], psum, x[:, :], ALU.add).then_inc(res_done, 1)
                else:
                    dve.scalar_tensor_tensor(x[:, :], psum, scale, x[:, :], ALU.mult, ALU.add).then_inc(res_done, 1)
                residuals[0] += 1
                dve.wait_ge(res_done, residuals[0])

            residuals = [0]
            dve.wait_ge(ld_x, 16)
            layernorm(0)
            dve.wait_ge(ld_const, 16)
            dve.tensor_copy(identb[:, :], ident)
            dve.tensor_copy(maskb[:, :, :], maskf.unsqueeze(1).broadcast_to([P, 4, P])).then_inc(consts_ready, 1)

            def rope(b):
                pairs = lambda t: t.rearrange("p j (i two) -> p j i two", two=2)
                link(dve.tensor_tensor(pairs(kvr[:, b]), pairs(ctxr[:, b]),
                                       rope_cos.unsqueeze(3).broadcast_to([P, J, 64, 2]), ALU.mult))
                dve.wait_ge(rope_swap, b + 1)
                dve.tensor_tensor(kvr[:, b], kvr[:, b], rope_tmp, ALU.add).then_inc(rope_ready, 1)

            def at_copy(g):
                dve.wait_ge(at_ps, g + 1)
                heads = qrk[0:R0, 4 * g:4 * g + 4, :].rearrange("p (j two) k -> p two j k", two=2)
                for odd in range(2):
                    ins = dve.tensor_copy(heads[:, odd], ps[odd * R0:odd * R0 + R0, 2 + g % 2, 0:2 * P].rearrange(
                        "p (j k) -> p j k", j=2))
                ins.then_inc(at_sb, 1)

            def bw_copy(g):
                dve.wait_ge(bw_ps, g + 1)
                dve.tensor_copy(qkw[:, 4 * g:4 * g + 4, :].rearrange("p h t -> p (h t)"), ps[:, 4 + g % 2, :]).then_inc(bw_sb, 1)

            def qk_copy(g):
                dve.wait_ge(qk_ps, g + 1)
                src = ps[:, 6, :].rearrange("p (h b s) -> p h b s", h=4, b=B)
                for b in range(B):
                    ins = dve.tensor_copy(qk_x[:, b, 4 * g:4 * g + 4, :], src[:, :, b, :])
                ins.then_inc(qk_sb, 1)

            at_copy(0)
            xT_copy(0)
            bw_copy(0)
            at_copy(1)
            qk_copy(0)
            bw_copy(1)
            dve.wait_ge(ld_ctx, 2 * 16)
            rope(0)
            rope(1)
            for g in range(2, GROUPS):
                at_copy(g)
                qk_copy(g - 1)
                bw_copy(g)
            qk_copy(GROUPS - 1)
            dve.wait_ge(c64T_ps, 1)
            dve.tensor_copy(ctx64T[:, :], ps[:, 7, 0:P]).then_inc(c64T_ready, 1)

            def row_max(u):
                dve.wait_ge(s_ps, u + 1)
                dve.tensor_reduce(mx_x[:, u:u + 1], ps[:, 2 * (u % 2):2 * (u % 2) + 2, :].rearrange("p a n -> p (a n)"),
                                  AX.X, ALU.max, negate=True).then_inc(mx_done, 1)

            def probT_copy(u):
                dve.wait_ge(pt_ps, 2 * u + 2)
                if u >= 2:
                    dve.wait_ge(ctx_ps, u - 1)
                dve.tensor_copy(probT_x[u % 2][:, 4:8, :].rearrange("p j r -> p (j r)"), ps[:, 5, :]).then_inc(pt_sb1, 1)

            def ctx_scale(u):
                dve.wait_ge(exp_done, u + 1)
                link(dve.reciprocal(rr_x[:, u:u + 1], rs_x[:, u:u + 1]))
                dve.wait_ge(ctx_ps, u + 1)
                if u >= 1:
                    dve.wait_ge(cT_ps, u)
                dve.tensor_scalar(xn[:, 0:P], ps[:, 6, 0:P], rr_x[:, u:u + 1], None, ALU.mult).then_inc(ctx_sb, 1)

            parts = [(0, 2048), (2048, 2560), (2560, 3072), (3072, 5120)]
            for i in range(UNITS + 2):
                if i < UNITS:
                    row_max(i)
                if 1 <= i <= UNITS:
                    probT_copy(i - 1)
                if i >= 2:
                    ctx_scale(i - 2)
                if 8 <= i < 12:
                    if i == 8:
                        dve.wait_ge(ld_e0, 16)
                    a0, a1 = parts[i - 8]
                    dve.tensor_reduce(asum[:, i - 8:i - 7], we[:, a0:a1], AX.X, ALU.add,
                                      apply_absolute_value=True).then_inc(asum_done, 1)
            for g in range(1, GROUPS, 2):
                dve.wait_ge(lat_ps, g + 1)
                dve.tensor_copy(latT[:, 4 * g:4 * g + 4, :].rearrange("p h t -> p (h t)"), ps[:, g, :]).then_inc(lat_sb1, 1)
            dve.wait_ge(wsum_ps, 1)
            for m, n in enumerate((D * D, P * D, P * D, D * D)):
                ins = dve.tensor_scalar(wscale[:, m:m + 1], ps[:, 5, m:m + 1], 1.0 / n, EPS, ALU.mult, ALU.max)
            link(ins)
            dve.scalar_tensor_tensor(sc_qk, wscale[:, 0:1], att_hd[0] ** -0.5, wscale[:, 1:2], ALU.mult, ALU.mult)
            dve.tensor_tensor(sc_vo, wscale[:, 2:3], wscale[:, 3:4], ALU.mult).then_inc(wscale_done, 1)
            dve.wait_ge(o_ps, 1)
            add_residual(ps[:, 4, :])

            def attention(a):
                n, hd, heads = att_banks[a], att_hd[a], att_kbd[a].shape[1]
                vw = att_v[a][:, 0:(heads) * (hd + 1)].rearrange("p (h e) -> p h e", e=hd + 1)

                def make_k():
                    dve.wait_ge(akv_ps[a], 1)
                    if a == 0:
                        ins = dve.tensor_tensor(att_kbd[0], ps[:, 1, 0:P].unsqueeze(1).broadcast_to([P, 8, P]),
                                                m16.unsqueeze(2).broadcast_to([P, 8, P]), ALU.mult)
                    else:
                        for c in range(4):
                            ins = dve.tensor_tensor(att_kbd[1][:, 4 * c:4 * c + 4],
                                                    ps[:, 1, c * P:(c + 1) * P].unsqueeze(1).broadcast_to([P, 4, P]),
                                                    m32.unsqueeze(2).broadcast_to([P, 4, P]), ALU.mult)
                    ins.then_inc(ak_sb[a], 1)

                def make_v():
                    link(dve.memset(att_v[a], 1.0))
                    dve.wait_ge(akv_ps[a], 2)
                    dve.tensor_copy(vw[:, :, 0:hd], ps[:, 2, 0:heads * hd].rearrange("p (h d) -> p h d", d=hd)).then_inc(av_sb[a], 1)

                if a == 1:
                    make_k()
                    make_v()
                layernorm(1 if a == 0 else 3)
                xT_copy(1 if a == 0 else 3)
                if a == 0:
                    make_k()
                    make_v()
                if a == 0:
                    o4 = att_o[0].rearrange("p (k g d) -> p g k d", k=8, g=4)
                    outs = [o4[:, i // 2, 4 * (i % 2):4 * (i % 2) + 4, :] for i in range(8)]
                else:
                    o4 = att_o[1].rearrange("p (i h d) -> p i h d", i=4, h=4)
                    outs = [o4[:, i] for i in range(4)]
                for i in range(n + 3):
                    if i < n:
                        dve.wait_ge(as_ps[a], i + 1)
                        s = ps[:, (3, 4, 2)[i % 3], :].rearrange("p (h t) -> p h t", h=4)
                        mx = att_mx[i % 2]
                        link(dve.tensor_reduce(mx, s, AX.X, ALU.max))
                        dve.tensor_tensor(att_prob[a][:, i], s, mx.unsqueeze(2).broadcast_to([P, 4, P]),
                                          ALU.subtract).then_inc(asub[a], 1)
                    if i >= 3:
                        m = i - 3
                        dve.wait_ge(ao_ps[a], m + 1)
                        o = ps[:, 7 if m % 2 == 0 else 0, :].rearrange("p (h t) -> p h t", h=4)
                        rec = att_rec[i % 2]
                        link(dve.reciprocal(rec, o[:, :, hd]))
                        dve.tensor_tensor(outs[m], o[:, :, 0:hd], rec.unsqueeze(2).broadcast_to([P, 4, hd]),
                                          ALU.mult).then_inc(ao_sb[a], 1)
                dve.wait_ge(aoT_ps[a], 1)
                dve.tensor_copy(att_oT[a].rearrange("p c t -> p (c t)"), ps[:, 1, :]).then_inc(aoT_sb[a], 1)
                dve.wait_ge(ap_ps[a], 1)
                add_residual(ps[:, 2, :], sc_vo if a == 0 else None)

            attention(0)

            layernorm(2)
            xT_copy(2)
            dve.wait_ge(r_ps, 1)
            dve.tensor_reduce(r_mx, ps[:, 0, 0:E0], AX.X, ALU.max, negate=True).then_inc(rmx_done, 1)
            dve.wait_ge(rexp_done, 1)
            link(dve.max(top8, r_e))
            link(dve.match_replace(r_rep, top8, r_e, -1.0))
            dve.tensor_tensor(r_sel, r_rep, r_e, ALU.not_equal).then_inc(sel_done, 1)
            link(dve.tensor_reduce(r_sum, top8, AX.X, ALU.add))
            link(dve.reciprocal(r_rec, r_sum))
            dve.wait_ge(sel_done, 1)
            link(dve.tensor_tensor(r_em, r_e, r_sel, ALU.mult))
            dve.wait_ge(pos_ps, 1)
            link(dve.scalar_tensor_tensor(r_place, ps[:, 1, 0:E0], 1.0, r_sel, ALU.add, ALU.mult))

            def place(e0, e1):
                n = e1 - e0
                dve.tensor_tensor(placed[:, e0:e1, :], iota[:, 1:CAP + 1].unsqueeze(1).broadcast_to([P, n, CAP]),
                                  r_place[:, 2 * DENSE + e0:2 * DENSE + e1].unsqueeze(2).broadcast_to([P, n, CAP]),
                                  ALU.is_equal).then_inc(places_done, 1)

            place(0, 4)
            link(dve.scalar_tensor_tensor(r_em, ps[:, 1, 0:E0], float(CAP), r_em, ALU.is_lt, ALU.mult))
            link(dve.tensor_scalar(coef, r_em, r_rec, 0.5, ALU.mult, ALU.mult))

            place(4, E0 - 2 * DENSE)

            def moe_hidden(p, k):
                dve.wait_ge(th_done, p + 1)
                link(dve.scalar_tensor_tensor(moe_a, moe_th[k], 1.0, ps[:, 2 + k, 0:384], ALU.add, ALU.mult))
                dve.wait_ge(u_ps, p + 1)
                for e in range(2):
                    for to, lo, hi in ((e * P, 0, P), (2 * P + e * 64, P, I0)):
                        ins = dve.scalar_tensor_tensor(moe_h[k][:, to:to + hi - lo], moe_a[:, e * I0 + lo:e * I0 + hi],
                                                       coef[:, 2 * p + e:2 * p + e + 1],
                                                       ps[:, 4 + k, e * I0 + lo:e * I0 + hi], ALU.mult, ALU.mult)
                ins.then_inc(h_done, 1)
                dve.wait_ge(h_done, p + 1)

            def moe_hidden_queued(p):
                dve.wait_ge(th_done, p + 1)
                link(dve.scalar_tensor_tensor(moe_a[:, 0:I0], moe_th[p % 2][:, 0:I0], 1.0, ps[:, 2 + p % 2, 0:I0],
                                              ALU.add, ALU.mult))
                if p >= DENSE + 2:
                    dve.wait_ge(hT_ps, p - 1)
                h, up = moe_hq[p % 2], ps[:, 2 + p % 2, I0:2 * I0]
                dve.tensor_tensor(h[:, 0:P], moe_a[:, 0:P], up[:, 0:P], ALU.mult)
                for e in range(2):
                    ins = dve.tensor_tensor(h[CAP * e:CAP * e + CAP, P + 64 * e:P + 64 * e + 64],
                                            moe_a[CAP * e:CAP * e + CAP, P:I0], up[CAP * e:CAP * e + CAP, P:I0], ALU.mult)
                ins.then_inc(h_done, 1)
                dve.wait_ge(h_done, p + 1)

            def moe_y_copy(p):
                dve.wait_ge(dn_done, p + 1)
                dve.tensor_copy(moe_y, ps[:, 4, :]).then_inc(y_sb, 1)

            for p in range(PAIRS):
                if p < DENSE:
                    moe_hidden(p, p % 2)
                else:
                    if p == DENSE:
                        dve.wait_ge(placed_w_done, 1)
                    moe_hidden_queued(p)
                if p > DENSE:
                    moe_y_copy(p - 1)
            moe_y_copy(PAIRS - 1)
            dve.wait_ge(moe_done, 1)
            add_residual(ps[:, 7, :])

            attention(1)

            layernorm(4)
            xT_copy(4)
            dve.wait_ge(t_ps, 2)
            dve.wait_ge(ld_late, late_loads * 16)
            qk = ps[:, 0:2, :]
            pairs_in = qk.rearrange("p t (n two) -> p t n two", two=2)
            pairs_tmp = rot_tmp.rearrange("p t (n two) -> p t n two", two=2)
            sin2 = xpos[:, 1, :].rearrange("p (n two) -> p n two", two=2)
            dve.tensor_tensor(rot, qk, xpos[:, 0:1, :].broadcast_to([P, 2, D]), ALU.mult)
            for k in range(2):
                ins = dve.tensor_tensor(pairs_tmp[:, :, :, k], pairs_in[:, :, :, 1 - k],
                                        sin2[:, :, k].unsqueeze(1).broadcast_to([P, 2, D // 2]), ALU.mult)
            link(ins)
            for t in range(2):
                dve.tensor_tensor(rot[:, t], rot[:, t], rot_tmp[:, t], ALU.add).then_inc(rot_done, 1)
            dve.wait_ge(ret_th_done, 1)
            dve.scalar_tensor_tensor(ret_ag, ret_th, 1.0, ps[:, 3, :], ALU.add, ALU.mult).then_inc(ag_done, 1)
            dve.wait_ge(ret_T_ps, 1)
            for c in range(C):
                dve.tensor_tensor(ret_qbd[:, c], ps[:, 4, c * P:(c + 1) * P].unsqueeze(1).broadcast_to([P, 4, P]),
                                  m32.unsqueeze(2).broadcast_to([P, 4, P]), ALU.mult).then_inc(qbd_done, 1)
            dve.wait_ge(ld_decay, 16)
            for c in range(C):
                dve.wait_ge(rs_ps, c + 1)
                dve.tensor_tensor(ret_pT[:, c].rearrange("p h t -> p (h t)"), ps[:, (6, 7, 0, 1)[c], :], decay[:, c, :],
                                  ALU.mult).then_inc(ret_pT_sb, 1)
            dve.wait_ge(ld_late, late_loads * 16)
            dve.wait_ge(ag_done, 1)
            link(dve.scalar_tensor_tensor(ret_aw, ret_ag, 0.5, gnwb[:, 0, :], ALU.mult, ALU.mult))
            link(dve.scalar_tensor_tensor(ret_ab, ret_ag, 0.5, gnwb[:, 1, :], ALU.mult, ALU.mult))
            dve.wait_ge(y_ps, C)
            y = ps[:, 4:8, :].rearrange("p c (h t) -> p (c h) t", h=4)[:, :, 0:32]
            link(dve.tensor_reduce(g_mean, y, AX.X, ALU.add))
            link(dve.scalar_tensor_tensor(ret_y, g_mean.unsqueeze(2).broadcast_to([P, 16, 32]), -1.0 / 32, y,
                                          ALU.mult, ALU.add))
            link(dve.tensor_tensor(ret_sq, ret_y, ret_y, ALU.mult))
            link(dve.tensor_reduce(g_var, ret_sq, AX.X, ALU.add))
            dve.tensor_scalar(g_var, g_var, 1.0 / 32, EPS, ALU.mult, ALU.add).then_inc(gvar_done, 1)
            yf = ret_y.rearrange("p h d -> p (h d)")
            link(dve.tensor_tensor(yf, yf, ret_aw, ALU.mult))
            dve.wait_ge(gsqrt_done, 1)
            link(dve.reciprocal(g_rstd[:, :], g_rstd[:, :]))
            link(dve.tensor_tensor(ret_y, ret_y, g_rstd[:, :].unsqueeze(2).broadcast_to([P, 16, 32]), ALU.mult))
            dve.tensor_tensor(yf, yf, ret_ab, ALU.add).then_inc(ret_o_done, 1)
            dve.wait_ge(ret_oT_ps, 1)
            dve.tensor_copy(ret_oT.rearrange("p c t -> p (c t)"), ps[:, 0, :]).then_inc(ret_oT_sb, 1)
            dve.wait_ge(ld_late, late_loads * 16)
            link(dve.tensor_tensor(amp[:, :, :], amp[:, :, :], amp[:, :, :], ALU.mult))
            link(dve.tensor_tensor(mix_p, amp[:, :, 0], amp[:, :, 1], ALU.add))
            link(dve.tensor_reduce(mix_s, mix_p, AX.X, ALU.add))
            link(dve.tensor_scalar(mix_s, mix_s, 1e-8, None, ALU.add))
            link(dve.reciprocal(mix_r, mix_s))
            dve.tensor_scalar(mix_w, mix_p, mix_r, None, ALU.mult).then_inc(mix_done, 1)
            dve.wait_ge(proj_ps, 1)
            add_residual(ps[:, 1, :])

            layernorm(5)
            xT_copy(5)
            dve.wait_ge(fr_ps, 1)
            dve.tensor_reduce(r_mx, ps[:, 0, 0:P], AX.X, ALU.max, negate=True).then_inc(frmx, 1)
            dve.wait_ge(frexp, 1)
            link(dve.max(top8, f1_e))
            link(dve.max_index(top8i[:, :], top8, f1_e))
            link(dve.tensor_copy(top8f, top8i[:, :]))
            link(dve.tensor_scalar(f1_sel, iota, top8f[:, 0:1], None, ALU.is_equal))
            for k in range(1, 4):
                link(dve.scalar_tensor_tensor(f1_sel, iota, top8f[:, k:k + 1], f1_sel, ALU.is_equal, ALU.add))
            link(dve.tensor_reduce(r_sum, top8[:, 0:4], AX.X, ALU.add))
            link(dve.scalar_tensor_tensor(r_sum, r_z, 1e-8, r_sum, ALU.mult, ALU.add))
            link(dve.reciprocal(r_rec, r_sum))
            link(dve.tensor_tensor(f1_sel, f1_sel, f1_e, ALU.mult))
            dve.wait_ge(ld_late, late_loads * 16)
            dve.scalar_tensor_tensor(f1_coef, f1_sel, r_rec, escale[:, :], ALU.mult, ALU.mult).then_inc(fcoef, 1)

            def f1_gated(n):
                dve.wait_ge(fth, n + 1)
                link(dve.scalar_tensor_tensor(f1_a, f1_th[n % 2], 1.0, ps[:, 1 + n % 2, :], ALU.add, ALU.mult))
                dve.wait_ge(fu_ps, n + 1)

            f1_gated(0)
            dve.scalar_tensor_tensor(f1_hs, f1_a, 0.5, ps[:, 3, :], ALU.mult, ALU.mult).then_inc(fh, 1)
            dve.wait_ge(fh, 1)
            dve.wait_ge(fcT_ps, 1)
            dve.tensor_copy(f1_coefT, ps[:, 0, 0:P]).then_inc(fcT_sb, 1)
            dve.wait_ge(fck_ps, 1)
            link(dve.tensor_scalar(ck, ps[:, 0, 0:8], 0.5, None, ALU.mult))
            for n in range(1, 5):
                f1_gated(n)
                for k in range(2):
                    kk = 2 * (n - 1) + k
                    ins = dve.scalar_tensor_tensor(f1_b[:, kk, :], f1_a[:, 256 * k:256 * k + 256], ck[:, kk:kk + 1],
                                                   ps[:, 3 + n % 2, 256 * k:256 * k + 256], ALU.mult, ALU.mult)
                ins.then_inc(fh, 1)
                dve.wait_ge(fh, n + 1)
            dve.wait_ge(fo_ps, 1)
            add_residual(ps[:, 7, :])

        @block.tensor
        def _(pe):
            def keep_clock(n, bank=6):
                idle = ones[:, :].bitcast(BF16)
                for _ in range(n):
                    pe.matmul(ps[:, bank, 0:256], idle[:, 0:P], idle, start=True, stop=True)

            def x_transposes(i):
                if i:
                    keep_clock(LN_WARM)
                pe.wait_ge(xn_ready, i + 1)
                src = xn[:, :].rearrange("p (q c) -> p c q", c=C)
                for c in range(C):
                    ins = pe.transpose(ps[:, 7, c * P:(c + 1) * P], src[:, c, :], ident)
                ins.then_inc(xT_ps, 1)

            def qrk_products(g):
                pe.wait_ge(ld_r[g], 16)
                if g >= 2:
                    pe.wait_ge(at_sb, g - 1)
                for j in range(2):
                    for c in range(KQ):
                        for odd in range(2):
                            h = 2 * j + odd
                            ins = pe.matmul(ps[odd * R0:odd * R0 + R0, 2 + g % 2, j * P:(j + 1) * P], wqr(g)[:, h, c, :],
                                            wkcq(g)[:, h, c, :], start=(c == 0), stop=(c == KQ - 1))
                ins.then_inc(at_ps, 1)

            def queries(g):
                pe.wait_ge(ld_q[g], 16)
                if g >= 2:
                    pe.wait_ge(q_sb, g - 1)
                for h in range(4):
                    for c in range(C):
                        ins = pe.matmul(ps[:, g % 2, h * P:(h + 1) * P], wq_x(g)[:, c, h * P:(h + 1) * P], xnT[:, c, :],
                                        start=(c == 0), stop=(c == C - 1))
                ins.then_inc(q_ps, 1)

            def context_transposes(g):
                if g == 0:
                    pe.wait_ge(xT_ready, 1)
                    pe.wait_ge(rope_ready, 1)
                else:
                    pe.wait_ge(kvT_sb, g)
                if g == 2:
                    pe.wait_ge(rope_ready, 2)
                for j in range(4):
                    ins = pe.transpose(ps[:, 7, j * P:(j + 1) * P], kvr[:, g // 2, 4 * (g % 2) + j, :], ident)
                ins.then_inc(kvT_ps, 1)

            def qkw_products(g):
                pe.wait_ge(at_sb, g + 1)
                if g == 0:
                    pe.wait_ge(ld_kr, 16)
                if g >= 2:
                    pe.wait_ge(bw_sb, g - 1)
                for h in range(4):
                    ins = pe.matmul(ps[:, 4 + g % 2, h * P:(h + 1) * P], qrk[0:R0, 4 * g + h, :], wkrT[0:R0, 4 * g + h, :],
                                    start=True, stop=True)
                ins.then_inc(bw_ps, 1)

            def latent_queries(g):
                pe.wait_ge(bw_sb, g + 1)
                pe.wait_ge(q_sb, g + 1)
                if g:
                    pe.wait_ge(qk_sb, g)
                for h in range(4):
                    ins = pe.matmul(ps[:, 6, h * P:(h + 1) * P], qkw[:, 4 * g + h, :], qT_x[:, 4 * g + h, :],
                                    start=True, stop=True)
                ins.then_inc(qk_ps, 1)

            pe.wait_ge(consts_ready, 1)
            keep_clock(44)
            qrk_products(0)
            pe.wait_ge(ld_const, 16)
            x_transposes(0)
            qkw_products(0)
            pe.wait_ge(xT_ready, 1)
            queries(0)
            for g in range(1, GROUPS):
                qrk_products(g)
                latent_queries(g - 1)
                if g > 1:
                    context_transposes(g - 2)
                qkw_products(g)
                if g == GROUPS - 1:
                    context_transposes(GROUPS - 2)
                queries(g)
            context_transposes(GROUPS - 1)
            latent_queries(GROUPS - 1)
            pe.wait_ge(kvT_sb, GROUPS)
            pe.wait_ge(ld_c64, 16)
            pe.transpose(ps[:, 7, 0:P], ctx64[:, :], ident).then_inc(c64T_ps, 1)

            def scores(u):
                if u == 0:
                    pe.wait_ge(qk_sb, GROUPS)
                if u >= 2:
                    pe.wait_ge(exp_done, u - 1)
                rows = qk_x[:, u % 2, 2 * (u // 2):2 * (u // 2) + 2, :].rearrange("p h s -> p (h s)")
                for half in range(2):
                    ins = pe.matmul(ps[:, 2 * (u % 2) + half, :], rows, kvT[:, u % 2, half * 512:half * 512 + 512],
                                    start=True, stop=True)
                ins.then_inc(s_ps, 1)

            def prob_transposes(u):
                pe.wait_ge(exp_done, u + 1)
                for half in range(2):
                    if u:
                        pe.wait_ge((pt_sb0, pt_sb1)[half], u)
                    for j in range(4):
                        ins = pe.transpose(ps[:, 4 + half, j * P:(j + 1) * P], prob_x[u % 2][:, 4 * half + j, :], ident)
                    ins.then_inc(pt_ps, 1)

            def context_products(u):
                pe.wait_ge(pt_sb0, u + 1)
                pe.wait_ge(pt_sb1, u + 1)
                if u:
                    pe.wait_ge(ctx_sb, u)
                for j in range(J):
                    ins = pe.matmul(ps[:, 6, 0:P], probT_x[u % 2][:, j, :], kvr[:, u % 2, j, :], start=(j == 0), stop=(j == J - 1))
                ins.then_inc(ctx_ps, 1)

            def result_transpose(u):
                pe.wait_ge(ctx_sb, u + 1)
                if u == 0:
                    pe.wait_ge(c64T_ready, 1)
                else:
                    pe.wait_ge(cT_sb, u)
                pe.transpose(ps[:, 7, 0:P], xn[:, 0:P], ident).then_inc(cT_ps, 1)

            def latent_values(g):
                pe.wait_ge(ld_b0, 16)
                pe.wait_ge(cT_sb, 4 * g + 4)
                for h in range(4 * g, 4 * g + 4):
                    ins = pe.matmul(ps[:, g, (h % 4) * P:(h % 4 + 1) * P], wkv_x[:, h, :],
                                    ctxT[:, h].rearrange("p b s -> p (b s)"), start=True, stop=True)
                ins.then_inc(lat_ps, 1)

            for i in range(UNITS + 3):
                if i < UNITS:
                    scores(i)
                if i == UNITS + 1:
                    latent_values(0)
                    latent_values(1)
                if i == UNITS + 2:
                    latent_values(2)
                if i >= 3:
                    result_transpose(i - 3)
                if 2 <= i < UNITS + 2:
                    context_products(i - 2)
                if 1 <= i <= UNITS:
                    prob_transposes(i - 1)
            def output_product(heads):
                pe.wait_ge(lat_sb0, heads[-1] // 8 + 1)
                if heads[-1] % 8 == 7:
                    pe.wait_ge(lat_sb1, heads[-1] // 8 + 1)
                for h in heads:
                    ins = pe.matmul(ps[:, 4, :], latT[:, h, :], wo_x[:, h, :], start=(h == 0), stop=(h == H0 - 1))
                return ins

            output_product(range(0, 4))
            output_product(range(4, 8))
            latent_values(3)
            pe.wait_ge(asum_done, 4)
            pe.wait_ge(consts_ready, 2)
            pe.matmul(ps[:, 5, 0:4], ones[:, :], asum, start=True, stop=True).then_inc(wsum_ps, 1)
            output_product(range(8, 12))
            output_product(range(12, 16)).then_inc(o_ps, 1)

            def attention(a):
                n, hd = att_banks[a], att_hd[a]
                ln = 1 if a == 0 else 3

                def keys_values():
                    if a == 0:
                        for c in range(C):
                            ins = pe.matmul(ps[:, 1, 0:P], e_wk0[:, c, :], xnT[:, c, :], start=(c == 0), stop=(c == C - 1))
                        ins.then_inc(akv_ps[a], 1)
                        for c in range(C):
                            ins = pe.matmul(ps[:, 2, 0:P], xnT[:, c, :], e_wv0[:, c, :], start=(c == 0), stop=(c == C - 1))
                        ins.then_inc(akv_ps[a], 1)
                    else:
                        pe.wait_ge(res_done, 3)
                        for c in range(4):
                            ins = pe.matmul(ps[:, 1, c * P:(c + 1) * P], e_wk1[:, c * P:(c + 1) * P], ctx64T[:, :],
                                            start=True, stop=True)
                        ins.then_inc(akv_ps[a], 1)
                        pe.matmul(ps[:, 2, :], ctx64T[:, :], e_wv1, start=True, stop=True).then_inc(akv_ps[a], 1)

                if a == 0:
                    pe.wait_ge(sign_done, 1)
                else:
                    pe.wait_ge(ld_e1, 16)
                    keys_values()
                x_transposes(ln)
                pe.wait_ge(xT_ready, ln + 1)
                if a == 0:
                    keys_values()
                for g in range(4):
                    for c in range(C):
                        ins = pe.matmul(ps[:, 0, g * P:(g + 1) * P], e_wq[:, c, g * P:(g + 1) * P], xnT[:, c, :],
                                        start=(c == 0), stop=(c == C - 1))
                ins.then_inc(aq_ps[a], 1)
                pe.wait_ge(consts_ready, 2)
                for i in range(n + 3):
                    if i < n:
                        if i == 0:
                            pe.wait_ge(aq_sb[a], 1)
                            pe.wait_ge(ak_sb[a], 1)
                        if i == 2:
                            pe.wait_ge(av_sb[a], 1)
                        if i >= 3:
                            pe.wait_ge(asub[a], i - 2)
                        if a == 0:
                            q, k = att_qT[0][:, i // 2, :], att_kbd[0][:, 4 * (i % 2):4 * (i % 2) + 4]
                        else:
                            q, k = att_qT[1][:, i, :], att_kbd[1][:, 4 * i:4 * i + 4]
                        bank = (3, 4, 2)[i % 3]
                        pe.matmul(ps[:, bank, :], q, k.rearrange("p h t -> p (h t)"), start=True, stop=False)
                        pe.matmul(ps[:, bank, :], identb[:, :], maskb[:, :, :].rearrange("p h t -> p (h t)"),
                                  start=False, stop=True).then_inc(as_ps[a], 1)
                    if i >= 3:
                        m = i - 3
                        pe.wait_ge(at2_sb[a], m + 1)
                        if m >= 2:
                            pe.wait_ge(ao_sb[a], m - 1)
                        for hh in range(4):
                            v0 = (4 * (m % 2) + hh if a == 0 else 4 * m + hh) * (hd + 1)
                            ins = pe.matmul(ps[:, 7 if m % 2 == 0 else 0, hh * P:hh * P + 97], att_probT[a][:, m, hh, :],
                                            att_v[a][:, v0:v0 + 97], start=True, stop=True)
                        ins.then_inc(ao_ps[a], 1)
                    if 2 <= i <= n + 1:
                        m = i - 2
                        pe.wait_ge(aexp[a], m + 1)
                        if m >= 2:
                            pe.wait_ge(at2_sb[a], m - 1)
                        for hh in range(4):
                            ins = pe.transpose(ps[:, 5 + m % 2, hh * P:(hh + 1) * P], att_prob[a][:, m, hh, :], ident)
                        ins.then_inc(at2_ps[a], 1)
                pe.wait_ge(ao_sb[a], n)
                src = att_o[a].rearrange("p (q c) -> p c q", c=C)
                for c in range(C):
                    ins = pe.transpose(ps[:, 1, c * P:(c + 1) * P], src[:, c, :], ident)
                ins.then_inc(aoT_ps[a], 1)
                pe.wait_ge(aoT_sb[a], 1)
                for c in range(C):
                    ins = pe.matmul(ps[:, 2, :], att_oT[a][:, c, :], e_wo[:, c, :], start=(c == 0), stop=(c == C - 1))
                ins.then_inc(ap_ps[a], 1)

            attention(0)

            x_transposes(2)
            pe.wait_ge(xT_ready, 3)
            pe.wait_ge(ld_gw, 16)
            for c in range(C):
                ins = pe.matmul(ps[:, 0, 0:E0], xnT[:, c, :], gatew[:, c, :], start=(c == 0), stop=(c == C - 1))
            ins.then_inc(r_ps, 1)

            def gate_up(p, j):
                pe.wait_ge(ld_ring[j], 16)
                for bank, w, done in ((2 + j % 2, slot_gate[j], g_ps), (4 + j % 2, slot_up[j], u_ps)):
                    for c in range(C):
                        ins = pe.matmul(ps[:, bank, 0:384].rearrange("p (e n) -> p e n", e=2), xnT[:, c, :], w[:, :, c, :],
                                        start=(c == 0), stop=(c == C - 1))
                    ins.then_inc(done, 1)

            def hidden_transposes(p, k):
                pe.wait_ge(h_done, p + 1)
                if p:
                    pe.wait_ge(hT_sb, p)
                for c in range(3):
                    ins = pe.transpose(ps[:, 6, c * P:(c + 1) * P], moe_h[k][:, c * P:(c + 1) * P], ident)
                ins.then_inc(hT_ps, 1)

            def down(p, j, first=False):
                pe.wait_ge(hT_sb, p + 1)
                for c in range(3):
                    ins = pe.matmul(ps[:, 7, :], moe_hT_even[j % 2][:, c, :], slot_down[j][:, c, :],
                                    start=(first and c == 0), stop=False)
                ins.then_inc(dn_done, 1)

            def gather(q, half):
                pe.wait_ge(places_done, min(q, 1) + 1)
                if q:
                    pe.wait_ge(xq_sb, 2 * (q - 1) + half + 1)
                src = xn[:, :].rearrange("p (q c) -> p c q", c=C)
                for c in range(2):
                    ins = pe.matmul(ps[:, half, c * 256:(c + 1) * 256], src[:, 2 * half + c, :],
                                    placed[:, 4 * q:4 * q + 4, :].rearrange("p e s -> p (e s)"), start=True, stop=True)
                ins.then_inc(xq_ps, 1)

            def gate_up_queued(p, j, turn):
                q = (p - DENSE) // 2
                pe.wait_ge(ld_ring[j], 16 * (turn + 1))
                pe.wait_ge(xq_sb, 2 * q + 2)
                pe.wait_ge(h_done, p - 1)
                for c in range(C):
                    for e in range(2):
                        e4 = 2 * (p % 2) + e
                        ins = pe.matmul(ps[CAP * e:CAP * e + CAP, 2 + p % 2, 0:2 * I0].rearrange("p (g n) -> p g n", g=2),
                                        moe_xq[q % 2][:, c, CAP * e4:CAP * e4 + CAP], slot_gu[j][:, :, e, c, :],
                                        start=(c == 0), stop=(c == C - 1))
                ins.then_inc(g_ps, 1)

            def hidden_transposes_queued(p):
                q = (p - DENSE) // 2
                pe.wait_ge(h_done, p + 1)
                pe.wait_ge(hT_sb, p)
                for c in range(2):
                    ins = pe.transpose(ps[:, 6, c * P:(c + 1) * P], moe_hq[p % 2][:, c * P:(c + 1) * P], ident)
                if p % 2 == 0:
                    pe.wait_ge(placed_w_done, q + 1)
                    for c in range(2):
                        ins = pe.transpose(ps[:, 6, (2 + c) * P:(3 + c) * P],
                                           placed_w[q % 2][:, 2 * c:2 * c + 2, :].rearrange("p e s -> p (e s)"), ident)
                ins.then_inc(hT_ps, 1)

            def down_queued(p, j):
                q = (p - DENSE) // 2
                hT = moe_hT_even[q % 2] if p % 2 == 0 else moe_hT_odd[q % 2]
                pe.wait_ge(hT_sb, p + 1)
                if p > DENSE:
                    pe.wait_ge(y_sb, p - DENSE)
                for e in range(2):
                    pe.matmul(ps[CAP * e:CAP * e + CAP, 4, :], hT[:, 0, CAP * e:CAP * e + CAP], slot_down[j][:, e, :],
                              start=True, stop=False)
                pe.matmul(ps[:, 4, :], hT[:, 1, :], slot_down[j][:, 2, :], start=False, stop=True).then_inc(dn_done, 1)

            def give_back(p, last=False):
                pe.wait_ge(y_sb, p - DENSE + 1)
                return pe.matmul(ps[:, 7, :], moe_hT_even[(p - DENSE) // 2 % 2][:, 2 + p % 2, :], moe_y,
                                 start=False, stop=last)

            gate_up(0, 0)
            pe.wait_ge(sel_done, 1)
            pe.matmul(ps[:, 1, 0:E0], upper, r_sel, start=True, stop=True).then_inc(pos_ps, 1)
            for p in range(1, PAIRS):
                if p < DENSE:
                    gate_up(p, p)
                else:
                    gate_up_queued(p, p % SLOTS, p // SLOTS)
                if p <= DENSE:
                    hidden_transposes(p - 1, (p - 1) % 2)
                else:
                    hidden_transposes_queued(p - 1)
                if p - 2 >= DENSE:
                    give_back(p - 2)
                if p == 1:
                    gather(0, 0)
                    gather(0, 1)
                elif p < PAIRS - 2:
                    gather(p // 2, p % 2)
                if p <= DENSE:
                    down(p - 1, p - 1, p == 1)
                else:
                    down_queued(p - 1, (p - 1) % SLOTS)
            hidden_transposes_queued(PAIRS - 1)
            give_back(PAIRS - 2)
            down_queued(PAIRS - 1, (PAIRS - 1) % SLOTS)
            give_back(PAIRS - 1, True).then_inc(moe_done, 1)

            attention(1)

            x_transposes(4)
            pe.wait_ge(xT_ready, 5)
            pe.wait_ge(ld_b1, 16)
            for t in range(4):
                for c in range(C):
                    ins = pe.matmul(ps[:, t, :], xnT[:, c, :], w_ret[:, c, t, :], start=(c == 0), stop=(c == C - 1))
                ins.then_inc(t_ps, 1)
            for t in range(2):
                pe.wait_ge(rot_done, t + 1)
                for c in range(C):
                    ins = pe.transpose(ps[:, 4 + t, c * P:(c + 1) * P], rot[:, t, c * P:(c + 1) * P], ident)
                ins.then_inc(ret_T_ps, 1)
            pe.wait_ge(ret_kT_sb, 1)
            for c in range(C):
                pe.wait_ge(qbd_done, c + 1)
                pe.matmul(ps[:, (6, 7, 0, 1)[c], :], ret_kT[:, c, :], ret_qbd[:, c].rearrange("p h t -> p (h t)"),
                          start=True, stop=True).then_inc(rs_ps, 1)
            pe.wait_ge(ret_v_sb, 1)
            for c in range(C):
                pe.wait_ge(ret_pT_sb, c + 1)
                for hh in range(4):
                    v0 = (4 * c + hh) * 32
                    ins = pe.matmul(ps[:, 4 + c, hh * P:hh * P + 96], ret_pT[:, c, hh, :], ret_v[:, v0:v0 + 96],
                                    start=True, stop=True)
                ins.then_inc(y_ps, 1)
            keep_clock(36, 3)
            pe.wait_ge(ret_o_done, 1)
            src = ret_y.rearrange("p h d -> p (h d)").rearrange("p (q c) -> p c q", c=C)
            for c in range(C):
                ins = pe.transpose(ps[:, 0, c * P:(c + 1) * P], src[:, c, :], ident)
            ins.then_inc(ret_oT_ps, 1)
            pe.wait_ge(ret_oT_sb, 1)
            for c in range(C):
                ins = pe.matmul(ps[:, 1, :], ret_oT[:, c, :], w_proj[:, c, :], start=(c == 0), stop=(c == C - 1))
            ins.then_inc(proj_ps, 1)

            x_transposes(5)
            pe.wait_ge(xT_ready, 6)
            pe.wait_ge(ld_router, 16)
            for c in range(C):
                ins = pe.matmul(ps[:, 0, 0:P], xnT[:, c, :], router[:, c, :], start=(c == 0), stop=(c == C - 1))
            ins.then_inc(fr_ps, 1)

            def f1_chunk(n):
                if n == 0:
                    pe.wait_ge(ld_f1s, 16)
                    gate, up = f1_sgate, f1_sup
                else:
                    pe.wait_ge(ld_f1[n - 1], 2 * 16)
                    gate, up = f1_gate[:, n - 1], f1_up[:, n - 1]
                if n >= 2:
                    pe.wait_ge(fh, n - 1)
                for bank, w, done in ((1 + n % 2, gate, fg_ps), (3 + n % 2, up, fu_ps)):
                    for c in range(C):
                        ins = pe.matmul(ps[:, bank, :], xnT[:, c, :], w[:, c, :], start=(c == 0), stop=(c == C - 1))
                    ins.then_inc(done, 1)

            f1_chunk(0)
            pe.wait_ge(fcoef, 1)
            pe.transpose(ps[:, 0, 0:P], f1_coef, ident).then_inc(fcT_ps, 1)
            f1_chunk(1)
            pe.wait_ge(fcT_sb, 1)
            pe.wait_ge(mix_done, 1)
            pe.matmul(ps[:, 0, 0:8], f1_coefT, mix_w, start=True, stop=True).then_inc(fck_ps, 1)
            pe.wait_ge(fh, 1)
            src = f1_hs.rearrange("p (q c) -> p c q", c=C)
            for c in range(C):
                ins = pe.transpose(ps[:, 5, c * P:(c + 1) * P], src[:, c, :], ident)
            ins.then_inc(fhT_ps, 1)
            f1_chunk(2)
            pe.wait_ge(fhT_sb, 1)
            pe.wait_ge(ld_f1d, 16)
            for c in range(C):
                pe.matmul(ps[:, 7, :], f1_hsT[:, c, :], f1_swd[:, c, :], start=(c == 0), stop=False)
            f1_chunk(3)
            f1_chunk(4)
            pe.wait_ge(fm_done, 1)
            src = f1_m.rearrange("p (q c) -> p c q", c=2)
            for c in range(2):
                ins = pe.transpose(ps[:, 6, c * P:(c + 1) * P], src[:, c, :], ident)
            ins.then_inc(fmT_ps, 1)
            pe.wait_ge(fmT_sb, 1)
            for c in range(2):
                ins = pe.matmul(ps[:, 7, :], f1_mT[:, c, :], f1_wd[:, c, :], start=False, stop=(c == 1))
            ins.then_inc(fo_ps, 1)


def constants():
    f = np.float32
    t = np.arange(P)
    same = t[:, None] // S == t[None, :] // S
    c = np.zeros((P, K_N), f)
    c[:, K_ID:K_ID + P] = np.eye(P)
    c[:, K_MASK:K_MASK + P] = np.where(same & (t[:, None] >= t[None, :]), 0.0, -1e30)
    c[:, K_U:K_U + P] = t[:, None] < t[None, :]
    c[:, K_IOTA:K_IOTA + P] = t[None, :]
    c[:, K_M16:K_M16 + 8] = t[:, None] // 16 == np.arange(8)[None, :]
    c[:, K_M32:K_M32 + 4] = t[:, None] // 32 == np.arange(4)[None, :]
    inv = (f(1.0) / np.power(f(10000.0), np.arange(0, P, 2, dtype=f) / f(P))).astype(f)
    fr = (np.arange(L, dtype=f)[:, None] * inv[None, :]).astype(f)
    cos, sin = np.cos(fr), np.sin(fr)
    sin[:, 0:P // 4] *= -1
    rope = np.concatenate([cos.reshape(P, -1), sin.reshape(P, -1)], axis=1).astype(f)
    ar = np.arange(0, D, 2, dtype=f)
    dim_scale = ((ar + f(0.4 * D)) / f(1.4 * D)).astype(f)
    pos = np.arange(S, dtype=f)
    scale = (dim_scale[None, :] ** (pos[:, None] / f(512.0))).astype(f)
    inv = (f(1.0) / np.power(f(10000.0), ar / f(D))).astype(f)
    sc = (pos[:, None] * inv[None, :]).astype(f)
    xs = np.repeat(np.sin(sc) * scale, 2, axis=-1)
    xc = np.repeat(np.cos(sc) * scale, 2, axis=-1)
    xs[:, 0::2] *= -1
    xpos = np.tile(np.concatenate([xc, xs], axis=1), (B, 1)).astype(f)
    gamma = (f(1.0) - f(2.0) ** (f(-5.0) - np.arange(16, dtype=f))).astype(f)
    diff = t[None, :] - t[:, None]
    ok = same & (diff >= 0)
    dec = np.where(ok[:, None, :], gamma[None, :, None] ** np.where(diff >= 0, diff, 0).astype(f)[:, None, :], f(0.0))
    decay = (dec.astype(f) * f(32.0) ** f(-0.5)).astype(f).reshape(P, 16 * P)
    return c, rope, xpos, decay


def kernel(**inputs):
    import concourse.bacc as _bacc
    from concourse.bass_utils import run_bass_kernel_spmd as _run

    v = {k: np.asarray(a) for k, a in inputs.items()}
    ac = np.ascontiguousarray
    cst, rope, xpos, decay = constants()
    wq = v["L0_xattn_Wq"].T.reshape(P, C, GROUPS, 512)
    wkcq = v["L0_xattn_w_kc_q"].transpose(2, 0, 1).reshape(P, KQ, H0, P)
    wqr = v["L0_xattn_W_qr"].transpose(1, 0, 2).reshape(P, KQ, H0, R0)
    wr = np.stack([np.concatenate([wkcq[:, :, 4 * g:4 * g + 4].transpose(0, 2, 1, 3).reshape(P, -1),
                                   wqr[:, :, 4 * g:4 * g + 4].transpose(0, 2, 1, 3).reshape(P, -1)], axis=1)
                   for g in range(GROUPS)])
    wq = wq.transpose(2, 0, 1, 3).reshape(GROUPS, P, -1)
    wkr = v["L0_xattn_W_kr"].transpose(2, 0, 1).reshape(R0, H0 * P)
    wb = np.concatenate([v["L0_xattn_Wo"].T.reshape(H0, P, D).transpose(1, 0, 2).reshape(P, -1),
                         v["L0_xattn_w_kc_kv"].transpose(2, 0, 1).reshape(P, -1)], axis=1)
    q0 = v["L0_attn_wq"].T.reshape(D, 8, 4, 16).transpose(0, 2, 1, 3).reshape(D, D)
    e0 = np.concatenate([q0.reshape(P, -1), v["L0_attn_wk"].T.reshape(P, -1), v["L0_attn_wv"].T.reshape(P, -1),
                         v["L0_attn_wo"].T.reshape(P, -1)], axis=1)
    pair = lambda w: w.reshape(PAIRS, 2, P, C, I0).transpose(0, 2, 1, 3, 4).reshape(PAIRS, P, -1)
    wd = v["L0_ffn_w_down"].reshape(PAIRS, 2, I0, D)
    down = np.stack([wd[:, 0, 0:P], wd[:, 1, 0:P], wd[:, :, P:I0].reshape(PAIRS, P, D)], axis=2)
    ring = np.concatenate([pair(v["L0_ffn_w_gate"]), pair(v["L0_ffn_w_up"]), down.reshape(PAIRS, P, 3 * D)], axis=2)
    kv1 = v["L1_xattn_Wkv_expand"].T
    e1 = np.concatenate([v["L1_xattn_Wq"].T.reshape(P, -1), kv1, v["L1_xattn_Wout"].T.reshape(P, -1)], axis=1)
    b1 = np.concatenate([np.concatenate([v["L1_attn_w_qkv"], v["L1_attn_w_g"]], axis=1).reshape(P, -1),
                         v["L1_attn_w_proj"].reshape(P, -1)], axis=1)
    gn = np.stack([v["L1_attn_gn_weight"], v["L1_attn_gn_bias"]])
    chunk = lambda w: w.reshape(P, C, 4, 512).transpose(2, 0, 1, 3)
    f1gu = np.concatenate([chunk(v["L1_ffn_w_gate"]), chunk(v["L1_ffn_w_up"])])
    f1s = np.concatenate([v["L1_ffn_shared_w_gate"].reshape(P, -1), v["L1_ffn_shared_w_up"].reshape(P, -1)], axis=1)
    f1d = np.concatenate([v["L1_ffn_w_down"].reshape(P, -1), v["L1_ffn_shared_w_down"].reshape(P, -1)], axis=1)
    ctx = v["ctx_512"]
    arrays = {
        "x": v["x"].reshape(P, D), "consts": cst, "rope": rope,
        "ctx": ctx.reshape(B, P, J * P).transpose(1, 0, 2).reshape(P, -1), "ctx64": ctx[:, 0:S].reshape(P, P),
        "wr": wr, "wq": wq, "wkr": wkr, "wb": wb, "e0": e0, "gatew": v["L0_ffn_gate_w"].reshape(P, -1), "ring": ring, "e1": e1,
        "b1": b1, "xpos": xpos, "gn": gn, "decay": decay, "f1gu": f1gu, "f1s": f1s, "f1d": f1d,
        "router": v["L1_ffn_w_router"].reshape(P, -1), "escale": v["L1_ffn_expert_scale"].reshape(1, P),
        "amp": v["L1_ffn_amplitudes"],
    }
    nc = _bacc.Bacc("TRN2", target_bir_lowering=False, num_devices=1)
    ins, args = {}, []
    for name, a in arrays.items():
        a = ac(a)
        ins[f"in_{name}"] = a
        args.append(nc.dram_tensor(f"in_{name}", a.shape, mybir.dt.from_np(a.dtype), kind="ExternalInput").ap())
    out = nc.dram_tensor("out_x", (P, D), F32, kind="ExternalOutput").ap()
    build(nc, *args, out)
    r = _run(nc, [ins], core_ids=[0])
    return r.results[0]["out_x"].reshape(B, S, D)
```
